# Optimizing a Trainium2 kernel written in Bass

```python
import numpy as np
import jax
import jax.numpy as jnp

def _softmax(x, axis=-1):
    return jax.nn.softmax(x, axis=axis)

def _gelu(x):
    return jax.nn.gelu(x, approximate=True)

def _silu(x):
    return jax.nn.silu(x)

def _sigmoid(x):
    return jax.nn.sigmoid(x)

def _layernorm(x, axis=-1, eps=1e-05):
    m = jnp.mean(x, axis=axis, keepdims=True)
    v = jnp.var(x, axis=axis, keepdims=True)
    return (x - m) / jnp.sqrt(v + eps)

def _scatter_add(tgt, idx, src, axis=0):
    return tgt.at[idx].add(src)

def _segment_sum(src, seg, n):
    return jax.ops.segment_sum(src, seg, n)
kernel_name = 'mk_hybrid_d1_jaxref_r4_710573'

def setup_inputs(seed: int=0):
    np.random.seed(seed)
    _w = jnp.asarray

    def _L0_attn_a_setup():
        import jax, jax.numpy as jnp
        import numpy as np
        D_MODEL, D_STATE, D_CONV, EXPAND = (256, 16, 4, 2)
        D_INNER = EXPAND * D_MODEL
        BATCH, LENGTH = (2, 256)

        def _mamba_fwd(x, in_proj_w, in_proj_b, conv_w, conv_b, x_proj_w, x_proj_b, dt_proj_w, dt_proj_b, D, out_proj_w, out_proj_b):
            batch, length, _ = x.shape
            d_inner = D.shape[0]
            d_state = dt_proj_w.shape[0]
            d_conv = conv_w.shape[-1]
            xz = x @ in_proj_w + in_proj_b
            xc, z = jnp.split(xz, 2, axis=-1)
            xc_bdl = jnp.transpose(xc, (0, 2, 1))
            xc_bdl = jax.lax.conv_general_dilated(xc_bdl, conv_w, window_strides=(1,), padding=[(d_conv - 1, 0)], dimension_numbers=('NCH', 'OIH', 'NCH'), feature_group_count=d_inner)
            xc_bdl = xc_bdl + conv_b[None, :, None]
            xc = jnp.transpose(xc_bdl, (0, 2, 1))
            xc = jax.nn.silu(xc)
            dBu = xc @ x_proj_w + x_proj_b
            delta_s, B, u = jnp.split(dBu, [d_state, 2 * d_state], axis=-1)
            delta = jax.nn.softplus(delta_s @ dt_proj_w + dt_proj_b)
            A = -jnp.arange(1, d_state + 1, dtype=x.dtype)
            deltaA = jnp.exp(delta[..., None] * A)
            deltaB_u = delta[..., None] * B[:, :, None, :] * u[..., None]
            dA_t = jnp.moveaxis(deltaA, 1, 0)
            dBu_t = jnp.moveaxis(deltaB_u, 1, 0)

            def step(h, inp):
                dA, dBu_ = inp
                h = dA * h + dBu_
                return (h, h.sum(-1))
            h0 = jnp.zeros((batch, d_inner, d_state), x.dtype)
            _, y_t = jax.lax.scan(step, h0, (dA_t, dBu_t))
            y = jnp.moveaxis(y_t, 0, 1)
            y = y + u * D
            y = y * jax.nn.silu(z)
            return y @ out_proj_w + out_proj_b
        key = jax.random.key(seed)
        ks = jax.random.split(key, 12)
        s = lambda fan_in: 1.0 / np.sqrt(fan_in)
        return {'x': jax.random.normal(ks[0], (BATCH, LENGTH, D_MODEL), jnp.float32), 'in_proj_w': jax.random.normal(ks[1], (D_MODEL, 2 * D_INNER), jnp.float32) * s(D_MODEL), 'in_proj_b': jax.random.normal(ks[2], (2 * D_INNER,), jnp.float32) * s(D_MODEL), 'conv_w': jax.random.normal(ks[3], (D_INNER, 1, D_CONV), jnp.float32) * s(D_CONV), 'conv_b': jax.random.normal(ks[4], (D_INNER,), jnp.float32) * s(D_CONV), 'x_proj_w': jax.random.normal(ks[5], (D_INNER, 2 * D_STATE + D_INNER), jnp.float32) * s(D_INNER), 'x_proj_b': jax.random.normal(ks[6], (2 * D_STATE + D_INNER,), jnp.float32) * s(D_INNER), 'dt_proj_w': jax.random.normal(ks[7], (D_STATE, D_INNER), jnp.float32) * s(D_STATE), 'dt_proj_b': jax.random.normal(ks[8], (D_INNER,), jnp.float32) * s(D_STATE), 'D': jnp.ones((D_INNER,), jnp.float32), 'out_proj_w': jax.random.normal(ks[9], (D_INNER, D_MODEL), jnp.float32) * s(D_INNER), 'out_proj_b': jax.random.normal(ks[10], (D_MODEL,), jnp.float32) * s(D_INNER)}
    _L0_attn_a_in = _L0_attn_a_setup()

    def _L0_attn_b_setup():
        import jax, jax.numpy as jnp
        import numpy as np
        D_MODEL = 256
        key = jax.random.key(seed)
        kx, kq, kk, kv = jax.random.split(key, 4)
        B, T, D = (4, 512, D_MODEL)
        bound = np.sqrt(6.0 / D) / np.sqrt(3.0)
        x = jax.random.normal(kx, (B, T, D), dtype=jnp.float32)
        w_q = jax.random.uniform(kq, (D, D), jnp.float32, -bound, bound)
        w_k = jax.random.uniform(kk, (D, D), jnp.float32, -bound, bound)
        w_v = jax.random.uniform(kv, (D, D), jnp.float32, -bound, bound)
        return {'x': x, 'w_q': w_q, 'w_k': w_k, 'w_v': w_v}
    _L0_attn_b_in = _L0_attn_b_setup()

    def _L0_ffn_setup():
        import jax, jax.numpy as jnp
        import numpy as np
        K = 2
        CAP_FACTOR = 1.25
        key = jax.random.key(seed)
        ks = jax.random.split(key, 6)
        B, T, C, H, E = (8, 512, 256, 1024, 8)
        return {'x': jax.random.normal(ks[0], (B, T, C), dtype=jnp.float32), 'Wr': jax.random.normal(ks[1], (C, E), dtype=jnp.float32) * 0.02, 'W1': jax.random.normal(ks[2], (E, C, H), dtype=jnp.float32) * 0.02, 'b1': jax.random.normal(ks[3], (E, H), dtype=jnp.float32) * 0.02, 'W2': jax.random.normal(ks[4], (E, H, C), dtype=jnp.float32) * 0.02, 'b2': jax.random.normal(ks[5], (E, C), dtype=jnp.float32) * 0.02}
    _L0_ffn_in = _L0_ffn_setup()
    _d = {'L0_attn_a_x': _L0_attn_a_in['x'], 'L0_attn_a_in_proj_w': _L0_attn_a_in['in_proj_w'], 'L0_attn_a_in_proj_b': _L0_attn_a_in['in_proj_b'], 'L0_attn_a_conv_w': _L0_attn_a_in['conv_w'], 'L0_attn_a_conv_b': _L0_attn_a_in['conv_b'], 'L0_attn_a_x_proj_w': _L0_attn_a_in['x_proj_w'], 'L0_attn_a_x_proj_b': _L0_attn_a_in['x_proj_b'], 'L0_attn_a_dt_proj_w': _L0_attn_a_in['dt_proj_w'], 'L0_attn_a_dt_proj_b': _L0_attn_a_in['dt_proj_b'], 'L0_attn_a_D': _L0_attn_a_in['D'], 'L0_attn_a_out_proj_w': _L0_attn_a_in['out_proj_w'], 'L0_attn_a_out_proj_b': _L0_attn_a_in['out_proj_b'], 'L0_attn_b_w_q': _L0_attn_b_in['w_q'], 'L0_attn_b_w_k': _L0_attn_b_in['w_k'], 'L0_attn_b_w_v': _L0_attn_b_in['w_v'], 'L0_ffn_Wr': _L0_ffn_in['Wr'], 'L0_ffn_W1': _L0_ffn_in['W1'], 'L0_ffn_b1': _L0_ffn_in['b1'], 'L0_ffn_W2': _L0_ffn_in['W2'], 'L0_ffn_b2': _L0_ffn_in['b2']}
    _x0 = _d['L0_attn_a_x']
    _d['L0_attn_a_x'] = jax.random.normal(jax.random.fold_in(jax.random.key(seed), 1), (16, 512, 256), dtype=_x0.dtype)
    del _x0
    return _d

def reference(L0_attn_a_x, L0_attn_a_in_proj_w, L0_attn_a_in_proj_b, L0_attn_a_conv_w, L0_attn_a_conv_b, L0_attn_a_x_proj_w, L0_attn_a_x_proj_b, L0_attn_a_dt_proj_w, L0_attn_a_dt_proj_b, L0_attn_a_D, L0_attn_a_out_proj_w, L0_attn_a_out_proj_b, L0_attn_b_w_q, L0_attn_b_w_k, L0_attn_b_w_v, L0_ffn_Wr, L0_ffn_W1, L0_ffn_b1, L0_ffn_W2, L0_ffn_b2):

    def _L0_attn_a_ref(x, in_proj_w, in_proj_b, conv_w, conv_b, x_proj_w, x_proj_b, dt_proj_w, dt_proj_b, D, out_proj_w, out_proj_b):
        import jax, jax.numpy as jnp
        import numpy as np
        D_MODEL, D_STATE, D_CONV, EXPAND = (256, 16, 4, 2)
        D_INNER = EXPAND * D_MODEL
        BATCH, LENGTH = (2, 256)

        def _mamba_fwd(x, in_proj_w, in_proj_b, conv_w, conv_b, x_proj_w, x_proj_b, dt_proj_w, dt_proj_b, D, out_proj_w, out_proj_b):
            batch, length, _ = x.shape
            d_inner = D.shape[0]
            d_state = dt_proj_w.shape[0]
            d_conv = conv_w.shape[-1]
            xz = x @ in_proj_w + in_proj_b
            xc, z = jnp.split(xz, 2, axis=-1)
            xc_bdl = jnp.transpose(xc, (0, 2, 1))
            xc_bdl = jax.lax.conv_general_dilated(xc_bdl, conv_w, window_strides=(1,), padding=[(d_conv - 1, 0)], dimension_numbers=('NCH', 'OIH', 'NCH'), feature_group_count=d_inner)
            xc_bdl = xc_bdl + conv_b[None, :, None]
            xc = jnp.transpose(xc_bdl, (0, 2, 1))
            xc = jax.nn.silu(xc)
            dBu = xc @ x_proj_w + x_proj_b
            delta_s, B, u = jnp.split(dBu, [d_state, 2 * d_state], axis=-1)
            delta = jax.nn.softplus(delta_s @ dt_proj_w + dt_proj_b)
            A = -jnp.arange(1, d_state + 1, dtype=x.dtype)
            deltaA = jnp.exp(delta[..., None] * A)
            deltaB_u = delta[..., None] * B[:, :, None, :] * u[..., None]
            dA_t = jnp.moveaxis(deltaA, 1, 0)
            dBu_t = jnp.moveaxis(deltaB_u, 1, 0)

            def step(h, inp):
                dA, dBu_ = inp
                h = dA * h + dBu_
                return (h, h.sum(-1))
            h0 = jnp.zeros((batch, d_inner, d_state), x.dtype)
            _, y_t = jax.lax.scan(step, h0, (dA_t, dBu_t))
            y = jnp.moveaxis(y_t, 0, 1)
            y = y + u * D
            y = y * jax.nn.silu(z)
            return y @ out_proj_w + out_proj_b
        return _mamba_fwd(x, in_proj_w, in_proj_b, conv_w, conv_b, x_proj_w, x_proj_b, dt_proj_w, dt_proj_b, D, out_proj_w, out_proj_b)

    def _L0_attn_b_ref(x, w_q, w_k, w_v):
        import jax, jax.numpy as jnp
        import numpy as np
        D_MODEL = 256
        B, T, D = x.shape
        q = jnp.einsum('btk,kd->btd', x, w_q)
        k = jnp.einsum('btk,kd->btd', x, w_k)
        v = jnp.einsum('btk,kd->btd', x, w_v)
        gamma = 1.0 / jnp.sqrt(jnp.float32(D))
        causal = jnp.tril(jnp.ones((T, T), dtype=bool))
        scores = jnp.einsum('bqd,bkd->bqk', q, k) * gamma
        scores = jnp.where(causal[None, :, :], scores, -jnp.inf)
        a = jax.nn.softmax(scores, axis=-1)
        y = jnp.einsum('bqt,btd->bqd', a, v)
        return y

    def _L0_ffn_ref(x, Wr, W1, b1, W2, b2):
        import jax, jax.numpy as jnp
        import numpy as np
        K = 2
        CAP_FACTOR = 1.25
        B, T, C = x.shape
        E = Wr.shape[1]
        capacity = int(T / E * CAP_FACTOR)
        probs = jax.nn.softmax(x @ Wr, axis=-1)
        topk_probs, topk_experts = jax.lax.top_k(probs, K)
        S = T * K
        e_flat = topk_experts.reshape(B, S)
        p_flat = topk_probs.reshape(B, S)
        x_rep = jnp.repeat(x, K, axis=1)
        onehot = jax.nn.one_hot(e_flat, E, dtype=jnp.int32)
        pos_all = jnp.cumsum(onehot, axis=1) - onehot
        pos = jnp.take_along_axis(pos_all, e_flat[..., None], axis=-1)[..., 0]
        keep = pos < capacity
        pos_c = jnp.minimum(pos, capacity - 1)
        b_idx = jnp.broadcast_to(jnp.arange(B)[:, None], (B, S))
        buf = jnp.zeros((E, B, capacity, C), dtype=x.dtype)
        buf = buf.at[e_flat, b_idx, pos_c].add(x_rep * keep[..., None].astype(x.dtype))
        h = jax.nn.relu(jnp.einsum('ebnc,ech->ebnh', buf, W1) + b1[:, None, None, :])
        y = jnp.einsum('ebnh,ehc->ebnc', h, W2) + b2[:, None, None, :]
        y_tok = y[e_flat, b_idx, pos_c]
        y_tok = y_tok * keep[..., None].astype(x.dtype) * p_flat[..., None]
        out = y_tok.reshape(B, T, K, C).sum(axis=2)
        return out
    x = L0_attn_a_x
    x = x + _L0_attn_a_ref(_layernorm(x, axis=-1), L0_attn_a_in_proj_w, L0_attn_a_in_proj_b, L0_attn_a_conv_w, L0_attn_a_conv_b, L0_attn_a_x_proj_w, L0_attn_a_x_proj_b, L0_attn_a_dt_proj_w, L0_attn_a_dt_proj_b, L0_attn_a_D, L0_attn_a_out_proj_w, L0_attn_a_out_proj_b)
    x = x + _L0_ffn_ref(_layernorm(x, axis=-1), L0_ffn_Wr, L0_ffn_W1, L0_ffn_b1, L0_ffn_W2, L0_ffn_b2)
    x = x + _L0_attn_b_ref(_layernorm(x, axis=-1), L0_attn_b_w_q, L0_attn_b_w_k, L0_attn_b_w_v)
    x = x + _L0_ffn_ref(_layernorm(x, axis=-1), L0_ffn_Wr, L0_ffn_W1, L0_ffn_b1, L0_ffn_W2, L0_ffn_b2)
    return x

_drawn_inputs = setup_inputs


def setup_inputs(seed=0):
    import zlib

    import numpy as np

    out = dict(_drawn_inputs(seed))
    spreads = {'L0_attn_a_D': (1.0, 0.2)}
    factors = {'L0_ffn_b1': 8.0, 'L0_ffn_b2': 8.0}
    for name, (base, spread) in spreads.items():
        noise = np.random.default_rng([zlib.crc32(name.encode()), seed]).standard_normal(out[name].shape)
        drawn = base * np.exp(spread * noise) if base else spread * noise
        out[name] = jnp.asarray(drawn.astype(out[name].dtype))
    for name, factor in factors.items():
        out[name] = (out[name] * factor).astype(out[name].dtype)
    return out
```

```python
from contextlib import ExitStack

import numpy as np
import concourse.bass as bass
from concourse import mybir

ACT = mybir.ActivationFunctionType
ALU = mybir.AluOpType
AX = mybir.AxisListType
F32 = mybir.dt.float32
BF16 = mybir.dt.bfloat16
F32R = mybir.dt.float32r
U32 = mybir.dt.uint32

P = 128
B, T, C = 16, 512, 256
NT, NC = T // P, C // P
DI, NS, DC = 512, 16, 4
ND = DI // P
E, H, K = 8, 1024, 2
NH = H // P
CAP = int(T / E * 1.25)
HALF = B // 2
ROWS = HALF * CAP
NR = ROWS // P
SLOTS = 2 * E * ROWS
EPS = 1e-5
FAR = float(2 * SLOTS)
RESET = 1.0e4

GN = 4
NG = NS // GN
SN = 2
STEPS = NS // SN * ND
DEEP = 4
ADDED = (5, 9, 16, 17, 18, 19, 20, 21, 22, 23, 26, 27)
XW = DI + 48


class Count:

    def __init__(self, sem, per, ahead=0):
        self.sem, self.per, self.ahead = sem, per, ahead

    def grant(self, eng):
        eng.sem_inc(self.sem, self.per * self.ahead)

    def at(self, row, n):
        value = (row + self.ahead) * self.per + n
        return max(value, 0) if isinstance(value, int) else value


LOGITS = 1
MASK = LOGITS + 2 * NT + 2
PLACES = MASK + 3
ROUTE_STEPS = PLACES + 9


class Router:

    def __init__(self, sb, sem, k, xbanks, lbank, pbank):
        self.k, self.xbanks, self.lbank, self.pbank = k, xbanks, lbank, pbank
        self.norm = Norm(sb, sem, k, "r_norm")
        self.xn, self.xnT = sb("r_xn", [P, NT, C]), sb("r_xnT", [P, NC, T])
        self.logits, self.best = sb("r_logits", [P, NT, E]), sb("r_best", [P, NT, 8])
        self.which, self.whichf = sb("r_which", [P, NT, 8], U32), sb("r_whichf", [P, NT, K])
        self.mask, self.maskb = sb("r_mask", [P, NT, K, E]), sb("r_maskb", [P, NT, E], BF16)
        self.below, self.e8 = sb("r_below", [P, NT, 8]), sb("r_e8", [P, NT, 8])
        self.esum, self.einv = sb("r_esum", [P, NT]), sb("r_einv", [P, NT])
        self.prob = sb("r_prob", [P, NT, K])
        self.mpos, self.pos = sb("r_mpos", [P, NT, K, E]), sb("r_pos", [P, NT, K])
        self.keep, self.cpos = sb("r_keep", [P, NT, K]), sb("r_cpos", [P, NT, K])
        self.slot, self.dead = sb("r_slot", [P, NT, K]), sb("r_dead", [P, NT, K])
        self.send = sb("r_send", [P, NT * K], U32)
        self.steps = Count(sem("r_steps"), ROUTE_STEPS)
        self.held = Count(sem("r_held"), 1)
        self.x_mm, self.x_ev = Count(sem("r_x_mm"), NC), Count(sem("r_x_ev"), NC)
        self.l_mm, self.p_mm = Count(sem("r_l_mm"), 1), Count(sem("r_p_mm"), 1)
        self.mask_ready = Count(sem("r_mask_ready"), 1)
        self.below_ready, self.e8_ready = Count(sem("r_below_ready"), 1), Count(sem("r_e8_ready"), 1)
        self.done = Count(sem("r_done"), 1)
        self.pool_held = Count(sem("r_pool_held"), 1)
        self.sent = Count(sem("r_sent"), 16 * NT * K)


class Norm:

    def __init__(self, sb, sem, k, name):
        self.k = k
        self.stats, self.ln = sb(name + "_stats", [P, NT, 6]), sb(name + "_ln", [P, 6, NT])
        self.steps = Count(sem(name + "_steps"), NT + 6)
        self.rstd_ready = Count(sem(name + "_rstd_ready"), 1)
        self.ready = Count(sem(name + "_ready"), NT)


def norm_stats(dve, n, x, row):
    done = n.steps
    for j in range(NT):
        dve.bn_stats(n.stats[:, j, :], x[:, j, :]).then_inc(done.sem, 1)
    me, m2e, mo, m2o = (n.stats[:, :, i] for i in (1, 2, 4, 5))
    total, diff, sq, mean, var = (n.ln[:, i, :] for i in range(5))
    dve.wait_ge(done.sem, done.at(row, NT))
    dve.tensor_tensor(total, me, mo, ALU.add).then_inc(done.sem, 1)
    dve.tensor_tensor(diff, me, mo, ALU.subtract).then_inc(done.sem, 1)
    dve.scalar_tensor_tensor(sq, m2e, C * EPS, m2o, ALU.add, ALU.add).then_inc(done.sem, 1)
    dve.wait_ge(done.sem, done.at(row, NT + 3))
    dve.tensor_scalar(mean, total, 0.5, None, ALU.mult).then_inc(done.sem, 1)
    dve.scalar_tensor_tensor(diff, diff, 0.25, diff, ALU.mult, ALU.mult).then_inc(done.sem, 1)
    dve.wait_ge(done.sem, done.at(row, NT + 5))
    dve.scalar_tensor_tensor(var, sq, 1.0 / C, diff, ALU.mult, ALU.add).then_inc(done.sem, 1)


def norm_rstd(pool, n, row):
    pool.wait_ge(n.steps.sem, n.steps.at(row, NT + 6))
    pool.tensor_tensor(n.ln[:, 5, :], n.ln[:, 4, :], n.k.minus_half[:], ALU.pow).then_inc(n.rstd_ready.sem, 1)


def norm_apply(dve, n, x, xn, row):
    dve.wait_ge(n.rstd_ready.sem, n.rstd_ready.at(row, 1))
    for j in range(NT):
        dve.tensor_scalar(xn[:, j, :], x[:, j, :], n.ln[:, 3, j:j + 1], n.ln[:, 5, j:j + 1],
                          ALU.subtract, ALU.mult).then_inc(n.ready.sem, 1)


def route_norm(dve, r, x, row):
    dve.wait_ge(r.sent.sem, r.sent.at(row - 1, 16 * NT * K))
    norm_apply(dve, r.norm, x, r.xn, row)


def route_transpose(pe, r, row, k):
    pe.wait_ge(r.norm.ready.sem, r.norm.ready.at(row, NT))
    for j in range(NT):
        mm = pe.transpose(r.xbanks[k][:, j * P:(j + 1) * P], r.xn[:, j, k * P:(k + 1) * P], r.k.ident[:])
    mm.then_inc(r.x_mm.sem, 1)


def route_turned(act, r, row, k):
    act.wait_ge(r.x_mm.sem, r.x_mm.at(row, k + 1))
    act.wait_ge(r.l_mm.sem, r.l_mm.at(row - 1, 1))
    act.activation(r.xnT[:, k, :], r.xbanks[k], ACT.Copy).then_inc(r.x_ev.sem, 1)


def route_logits(pe, r, row):
    pe.wait_ge(r.x_ev.sem, r.x_ev.at(row, NC))
    pe.wait_ge(r.done.sem, r.done.at(row - 1, 1))
    for j in range(NT):
        for k in range(NC):
            mm = pe.matmul(r.lbank[:, j * E:(j + 1) * E], r.xnT[:, k, j * P:(j + 1) * P], r.k.w_router[:, k, :],
                           start=(k == 0), stop=(k == NC - 1))
    mm.then_inc(r.l_mm.sem, 1)


def route_best(dve, r, row):
    done = r.steps
    dve.wait_ge(r.l_mm.sem, r.l_mm.at(row, 1))
    dve.tensor_copy(r.logits[:], r.lbank[:, 0:NT * E].rearrange("p (j e) -> p j e", e=E)).then_inc(done.sem, 1)
    dve.wait_ge(done.sem, done.at(row, LOGITS))
    dve.sem_inc(r.held.sem, 1)
    for j in range(NT):
        dve.max(r.best[:, j, :], r.logits[:, j, :]).then_inc(done.sem, 1)
    dve.wait_ge(done.sem, done.at(row, LOGITS + NT))
    dve.sem_inc(r.held.sem, 1)
    for j in range(NT):
        dve.max_index(r.which[:, j, :], r.best[:, j, :], r.logits[:, j, :]).then_inc(done.sem, 1)
    dve.wait_ge(r.e8_ready.sem, r.e8_ready.at(row - 1, 1))
    dve.tensor_tensor(r.below[:], r.best[:], r.best[:, :, 0:1].to_broadcast([P, NT, 8]),
                      ALU.subtract).then_inc(r.below_ready.sem, 1)
    dve.wait_ge(done.sem, done.at(row, LOGITS + 2 * NT))
    dve.tensor_copy(r.whichf[:], r.which[:, :, 0:K]).then_inc(done.sem, 1)
    dve.wait_ge(done.sem, done.at(row, LOGITS + 2 * NT + 1))
    dve.tensor_tensor(r.mask[:], r.k.iota_e[:].unsqueeze(1).unsqueeze(1).to_broadcast([P, NT, K, E]),
                      r.whichf[:].unsqueeze(3).to_broadcast([P, NT, K, E]), ALU.is_equal).then_inc(done.sem, 1)
    dve.wait_ge(done.sem, done.at(row, MASK))
    dve.tensor_tensor(r.maskb[:], r.mask[:, :, 0, :], r.mask[:, :, 1, :], ALU.add).then_inc(r.mask_ready.sem, 1)


def route_exp(act, r, row):
    act.wait_ge(r.below_ready.sem, r.below_ready.at(row, 1))
    act.wait_ge(r.done.sem, r.done.at(row - 1, 1))
    act.activation(r.e8[:], r.below[:], ACT.Exp).then_inc(r.e8_ready.sem, 1)


def route_places(pe, r, row):
    pe.wait_ge(r.mask_ready.sem, r.mask_ready.at(row, 1))
    for j in range(NT):
        for i in range(j + 1):
            mm = pe.matmul(r.pbank[:, j * E:(j + 1) * E], r.k.ones[:] if i < j else r.k.earlier[:], r.maskb[:, i, :],
                           start=(i == 0), stop=(i == j))
    mm.then_inc(r.p_mm.sem, 1)


def route_slots(dve, r, row):
    done = r.steps
    dve.wait_ge(r.e8_ready.sem, r.e8_ready.at(row, 1))
    dve.tensor_reduce(r.esum[:], r.e8[:], AX.X, ALU.add).then_inc(done.sem, 1)
    dve.wait_ge(done.sem, done.at(row, MASK + 1))
    dve.reciprocal(r.einv[:], r.esum[:]).then_inc(done.sem, 1)
    dve.wait_ge(r.p_mm.sem, r.p_mm.at(row, 1))
    places = r.pbank[:, 0:NT * E].rearrange("p (j e) -> p j e", e=E).unsqueeze(2).to_broadcast([P, NT, K, E])
    dve.tensor_tensor(r.mpos[:], r.mask[:], places, ALU.mult).then_inc(done.sem, 1)
    dve.wait_ge(done.sem, done.at(row, MASK + 2))
    dve.tensor_tensor(r.prob[:], r.e8[:, :, 0:K], r.einv[:].unsqueeze(2).to_broadcast([P, NT, K]),
                      ALU.mult).then_inc(done.sem, 1)
    dve.wait_ge(done.sem, done.at(row, PLACES))
    dve.tensor_reduce(r.pos[:], r.mpos[:], AX.X, ALU.add).then_inc(done.sem, 1)
    dve.wait_ge(done.sem, done.at(row, PLACES + 2))
    dve.tensor_scalar(r.keep[:], r.pos[:], float(CAP), None, ALU.is_lt).then_inc(done.sem, 1)
    dve.tensor_scalar(r.cpos[:], r.pos[:], float(CAP - 1), None, ALU.min).then_inc(done.sem, 1)
    dve.tensor_scalar(r.dead[:], r.pos[:], float(CAP), FAR, ALU.is_ge, ALU.mult).then_inc(done.sem, 1)
    dve.wait_ge(done.sem, done.at(row, PLACES + 5))
    dve.scalar_tensor_tensor(r.slot[:], r.whichf[:], float(ROWS), r.cpos[:], ALU.mult, ALU.add).then_inc(done.sem, 1)
    base = r.k.row_base[:, bass.ds(row, 1)].unsqueeze(2).to_broadcast([P, NT, K])
    dve.wait_ge(done.sem, done.at(row, PLACES + 6))
    dve.tensor_tensor(r.slot[:], r.slot[:], base, ALU.add).then_inc(done.sem, 1)
    share = r.k.share[:, bass.ds(row, 1), :].rearrange("p a (j k) -> p (a j) k", k=K)
    fetch = r.k.fetch[:, bass.ds(row, 1), :].rearrange("p a (j k) -> p (a j) k", k=K)
    dve.tensor_tensor(share, r.prob[:], r.keep[:], ALU.mult).then_inc(done.sem, 1)
    dve.wait_ge(done.sem, done.at(row, PLACES + 7))
    dve.tensor_copy(fetch, r.slot[:]).then_inc(done.sem, 1)
    dve.tensor_tensor(r.send[:].rearrange("p (j k) -> p j k", k=K), r.slot[:], r.dead[:],
                      ALU.add).then_inc(r.done.sem, 1)


def route_send(pool, r, row, n):
    if n == 0:
        pool.wait_ge(r.done.sem, r.done.at(row, 1))
        pool.sem_inc(r.pool_held.sem, 1)
    pool.indirect_dma_start(
        r.k.slots, bass.IndirectOffsetOnAxis(ap=r.send[:, n:n + 1], axis=0), r.xn[:, n // K, :], None,
        bounds_check=SLOTS - 1, oob_is_err=False).then_inc(r.sent.sem, 16)


class Kit:
    pass


def columns(ap):
    return ap.rearrange("(m p) -> p m", p=P)


def build_kit(nc, ctx, w):
    k = Kit()

    def sb(name, shape, dt=F32):
        return ctx.enter_context(nc.sbuf_tensor(name, shape, dt))

    def sem(name):
        return ctx.enter_context(nc.semaphore(name))

    k.ident, k.identb = sb("ident", [P, P]), sb("identb", [P, P], BF16)
    k.earlier, k.ones = sb("earlier", [P, P], BF16), sb("ones", [P, P], BF16)
    k.future = sb("future", [P, T], BF16)
    k.iota_e, k.row_base = sb("iota_e", [P, E]), sb("row_base", [P, B])
    k.minus_half = sb("minus_half", [P, NT])
    k.w_router = sb("w_router", [P, NC, E])
    k.b1 = sb("b1", [P, 2 * E, NH])
    k.share, k.fetch = sb("share", [P, B, NT * K]), sb("fetch", [P, B, NT * K], U32)
    zero = sb("zero", [P, 4 * C])

    def dram(name, shape):
        return nc.dram_tensor(name, shape, F32, kind="Internal").ap()

    k.slots, k.results = dram("slots", (SLOTS, C)), dram("results", (SLOTS, C))
    k.x1, k.x3 = dram("x_after_mamba", (B, T, C)), dram("x_after_attention", (B, T, C))
    k.b_rows = dram("b_rows", (2, NS, T))
    made, shaped, loaded, zeroed = sem("made"), sem("shaped"), sem("kit_loaded"), sem("slots_zeroed")
    zero_ready = sem("zero_ready")

    with nc.Block() as block:
        @block.gpsimd
        def _(pool):
            for t, v in ((k.ident, 0.0), (k.identb, 0.0), (k.earlier, 0.0), (k.ones, 1.0), (k.future, 0.0),
                         (k.minus_half, -0.5)):
                pool.memset(t[:], v).then_inc(made, 1)
            pool.memset(zero[:], 0.0).then_inc(zero_ready, 1)
            pool.wait_ge(made, 6)
            for t in (k.ident, k.identb):
                pool.affine_select(out=t[:], in_=t[:], compare_op=ALU.not_equal, fill=1.0, base=0,
                                   pattern=[[-1, P]], channel_multiplier=1).then_inc(shaped, 1)
            pool.affine_select(out=k.earlier[:], in_=k.earlier[:], compare_op=ALU.is_ge, fill=1.0, base=0,
                               pattern=[[-1, P]], channel_multiplier=1).then_inc(shaped, 1)
            pool.affine_select(out=k.future[:, T - P:], in_=k.future[:, T - P:], compare_op=ALU.is_ge, fill=-1.0e30, base=0,
                               pattern=[[-1, P]], channel_multiplier=1).then_inc(shaped, 1)
            pool.iota(k.iota_e[:], [[1, E]], base=0, channel_multiplier=0,
                      allow_small_or_imprecise_dtypes=True).then_inc(shaped, 1)
            pool.iota(k.row_base[:], [[E * ROWS, 2], [CAP, HALF]], base=0, channel_multiplier=0,
                      allow_small_or_imprecise_dtypes=True).then_inc(shaped, 1)
            pool.wait_ge(shaped, 6)

        @block.sync
        def _(sp):
            sp.dma_start(k.w_router[:], w["Wr"].rearrange("(k p) e -> p k e", p=P)).then_inc(loaded, 16)
            for turn in range(2 * E):
                sp.dma_start(k.b1[:, turn, :], columns(w["b1"][turn % E])).then_inc(loaded, 16)
            sp.wait_ge(zero_ready, 1)
            per = 4 * P
            for i in range(SLOTS // per):
                sp.dma_start(k.slots[i * per:(i + 1) * per].rearrange("(p r) c -> p (r c)", p=P),
                             zero[:]).then_inc(zeroed, 16)
            sp.wait_ge(loaded, 16 * (1 + 2 * E))
            sp.wait_ge(zeroed, 16 * (SLOTS // per))
    return k


def mamba_phase(nc, k, w):
    with ExitStack() as ctx:
        def sb(name, shape, dt=F32):
            return ctx.enter_context(nc.sbuf_tensor(name, shape, dt))

        def sem(name):
            return ctx.enter_context(nc.semaphore(name))

        w_in, w_x = sb("w_in", [P, NC, 2 * DI]), sb("w_x", [P, ND, XW])
        w_dt, w_out = sb("w_dt", [32, DI]), sb("w_out", [P, ND, C])
        b_in, b_z, b_u = sb("b_in", [P, 2 * ND]), sb("b_z", [P, ND]), sb("b_u", [P, ND])
        b_db, w_conv, b_conv = sb("b_db", [48, 1]), sb("w_conv", [P, ND, DC]), sb("b_conv", [P, ND])
        d_skip, b_out = sb("d_skip", [P, ND]), sb("b_out", [P, C])
        xt, xnT = sb("xt", [P, NT, C]), sb("xnT", [P, NC, T])
        norm = Norm(sb, sem, k, "norm")
        xc = sb("xc", [P, ND, DC - 1 + T])
        hx, th = sb("hx", [P, ND, T]), sb("th", [P, 2, T])
        db = sb("db", [48, T])
        delta, du, u = (sb(n, [P, 2, ND, T]) for n in ("delta", "du", "u"))
        sz = sb("sz", [P, 2, ND, T])
        bb = sb("bb", [P, 2, GN, T])
        da, dbu, hs = (sb(n, [P, DEEP, SN, T]) for n in ("da", "dbu", "hs"))
        x1 = sb("x1", [P, NT, C])
        ys = ctx.enter_context(nc.psum_tensor("ys", [P, ND, T], F32))
        ring = ctx.enter_context(nc.psum_tensor("ring", [P, 2, T], F32))
        ob = ctx.enter_context(nc.psum_tensor("ob", [P, 2, T], F32))
        tail_of_xc = xc[:, :, DC - 1:]

        r = Router(sb, sem, k, [ob[:, 0, :], ob[:, 1, :]], ob[:, 0, :], ob[:, 1, :])

        loaded, cleared, dt_cleared, halved = sem("loaded"), sem("cleared"), sem("dt_cleared"), sem("halved")
        bias_one = sem("bias_one")
        x_ld, x1_ld, x1_st = Count(sem("x_ld"), 16), Count(sem("x1_ld"), 16), Count(sem("x1_st"), 16)
        b_st, sp_held = Count(sem("b_st"), 16), sem("sp_held")
        bb_ld = [Count(sem(f"bb_ld{g}"), 16) for g in range(NG)]
        x1_based = Count(sem("x1_based"), 1)
        TJ, IJ, SJ = 0, NC, NC + ND
        DJ = SJ + 2
        UJ = [SJ + 1] + [DJ + ND + m for m in range(ND - 1)]
        ZJ = UJ[-1] + 1
        JOBS = ZJ + ND
        job_mm, job_ev = Count(sem("job_mm"), JOBS), Count(sem("job_ev"), JOBS)
        thx_ready, xc_ready = Count(sem("thx_ready"), ND), Count(sem("xc_ready"), ND)
        thz_ready, sz_ready = Count(sem("thz_ready"), ND), Count(sem("sz_ready"), ND)
        conv = Count(sem("conv"), ND * DC)
        exp_done, log_done = Count(sem("exp_done"), 1), Count(sem("log_done"), 1)
        delta_ready, du_ready = Count(sem("delta_ready"), ND), Count(sem("du_ready"), ND)
        reset_ready = Count(sem("reset_ready"), ND)
        da_ready, dbu_ready = Count(sem("da_ready"), STEPS), Count(sem("dbu_ready"), STEPS)
        scanned, summed = Count(sem("scanned"), STEPS), Count(sem("summed"), STEPS)
        added = Count(sem("added"), len(ADDED))
        ys_read, y2_ready = Count(sem("ys_read"), ND), Count(sem("y2_ready"), ND)
        o_mm, x1_ready = Count(sem("o_mm"), 2), Count(sem("x1_ready"), 2)

        CONSTS = 15

        def load_consts(sp):
            ws = [(w_in[:], w["in_proj_w"].rearrange("(k p) n -> p k n", p=P)),
                  (w_x[:, :, 0:DI], w["x_proj_w"][:, 2 * NS:].rearrange("(k p) n -> p k n", p=P)),
                  (w_x[:, :, DI:DI + NS], w["x_proj_w"][:, 0:NS].rearrange("(k p) n -> p k n", p=P)),
                  (w_x[:, :, DI + 32:], w["x_proj_w"][:, NS:2 * NS].rearrange("(k p) n -> p k n", p=P)),
                  (w_out[:], w["out_proj_w"].rearrange("(k p) n -> p k n", p=P)),
                  (b_in[:], columns(w["in_proj_b"])), (b_u[:], columns(w["x_proj_b"][2 * NS:])),
                  (w_conv[:], w["conv_w"].rearrange("(m p) a k -> p m (a k)", p=P)),
                  (b_conv[:], columns(w["conv_b"])), (d_skip[:], columns(w["D"])),
                  (b_out[:], w["out_proj_b"].partition_broadcast(P))]
            for dst, src in ws:
                sp.dma_start(dst, src).then_inc(loaded, 16)
            sp.wait_ge(dt_cleared, 1)
            sp.dma_start(w_dt[0:NS, :], w["dt_proj_w"]).then_inc(loaded, 16)
            sp.dma_start(w_dt[NS:NS + 1, :], w["dt_proj_b"].rearrange("(a n) -> a n", a=1)).then_inc(loaded, 16)
            sp.wait_ge(bias_one, 2)
            sp.dma_start(b_db[0:NS, :], w["x_proj_b"][0:NS].rearrange("(n a) -> n a", a=1)).then_inc(loaded, 16)
            sp.dma_start(b_db[32:48, :], w["x_proj_b"][NS:2 * NS].rearrange("(n a) -> n a", a=1)).then_inc(loaded, 16)

        def load_x(sp, row):
            sp.wait_ge(job_mm.sem, job_mm.at(row - 1, TJ + NC))
            sp.dma_start(xt[:], w["x"][row].rearrange("(j p) c -> p j c", p=P)).then_inc(x_ld.sem, 16)

        def load_x1(sp, row):
            sp.wait_ge(r.norm.ready.sem, r.norm.ready.at(row - 1, NT))
            sp.wait_ge(x1_st.sem, x1_st.at(row - 1, 16))
            sp.dma_start(x1[:], w["x"][row].rearrange("(j p) c -> p j c", p=P)).then_inc(x1_ld.sem, 16)

        def store_x1(sp, row):
            sp.wait_ge(x1_ready.sem, x1_ready.at(row, 2))
            sp.dma_start(k.x1[row].rearrange("(j p) c -> p j c", p=P), x1[:]).then_inc(x1_st.sem, 16)

        def store_b(sp, row, par):
            sp.wait_ge(job_ev.sem, job_ev.at(row, SJ + 1))
            sp.dma_start(k.b_rows[par], db[32:48, :]).then_inc(b_st.sem, 16)

        def spread_b(sp, row, par, g):
            if g == 0:
                sp.wait_ge(b_st.sem, b_st.at(row, 16))
                sp.sem_inc(sp_held, 1)
            sp.wait_ge(dbu_ready.sem, dbu_ready.at(row, (g - 1) * STEPS // NG))
            src = k.b_rows[par, g * GN:(g + 1) * GN, :].rearrange("n t -> (n t)").partition_broadcast(P)
            sp.dma_start(bb[:, g % 2].rearrange("p n t -> p (n t)"), src).then_inc(bb_ld[g].sem, 16)

        def add_out_bias(pool, row):
            pool.wait_ge(x1_ld.sem, x1_ld.at(row, 16))
            pool.tensor_tensor(x1[:], x1[:], b_out[:].unsqueeze(1).to_broadcast([P, NT, C]),
                               ALU.add).then_inc(x1_based.sem, 1)

        def step_of(s):
            return s // (STEPS // NG), s % (STEPS // NG) // (GN // SN), s % (GN // SN)

        def input_step(pool, row, par, s):
            g, dt, part = step_of(s)
            if g == 0 and part == 0:
                pool.wait_ge(du_ready.sem, du_ready.at(row, dt + 1))
            if dt == 0 and part == 0:
                pool.wait_ge(bb_ld[g].sem, bb_ld[g].at(row, 16))
            pool.wait_ge(scanned.sem, scanned.at(row, s + 1 - DEEP))
            pool.tensor_tensor(dbu[:, s % DEEP], du[:, par, dt, :].unsqueeze(1).to_broadcast([P, SN, T]),
                               bb[:, g % 2, part * SN:(part + 1) * SN, :], ALU.mult).then_inc(dbu_ready.sem, 1)

        def turned(act, row, par, c):
            act.wait_ge(job_mm.sem, job_mm.at(row, TJ + c + 1))
            act.activation(xnT[:, c, :], ring[:, (par + TJ + c) % 2, :], ACT.Copy).then_inc(job_ev.sem, 1)

        def conv_input(act, row, par, m):
            act.wait_ge(job_mm.sem, job_mm.at(row, IJ + m + 1))
            act.wait_ge(delta_ready.sem, delta_ready.at(row - 1, ND))
            act.activation(xc[:, m, DC - 1:], ring[:, (par + IJ + m) % 2, :], ACT.Identity,
                           bias=b_in[:, m:m + 1]).then_inc(job_ev.sem, 1)

        def tanh_x(act, row, m):
            act.wait_ge(conv.sem, conv.at(row, DC * (m + 1)))
            if m < 2:
                act.wait_ge(sz_ready.sem, sz_ready.at(row - 1, m + 3))
            else:
                act.wait_ge(xc_ready.sem, xc_ready.at(row, m - 1))
            act.activation(th[:, m % 2, :], hx[:, m, :], ACT.Tanh).then_inc(thx_ready.sem, 1)

        def gate_input(act, row, par, m):
            act.wait_ge(job_mm.sem, job_mm.at(row, ZJ + m + 1))
            act.wait_ge(o_mm.sem, o_mm.at(row - 2, 2))
            act.activation(sz[:, par, m, :], ring[:, (par + ZJ + m) % 2, :], ACT.Identity, bias=b_z[:, m:m + 1],
                           scale=0.5).then_inc(job_ev.sem, 1)

        def tanh_z(act, row, par, m):
            act.wait_ge(job_ev.sem, job_ev.at(row, ZJ + m + 1))
            if m < 2:
                act.wait_ge(xc_ready.sem, xc_ready.at(row, m + 3))
            else:
                act.wait_ge(sz_ready.sem, sz_ready.at(row, m - 1))
            act.activation(th[:, m % 2, :], sz[:, par, m, :], ACT.Tanh).then_inc(thz_ready.sem, 1)

        def delta_b(act, row, par):
            act.wait_ge(job_mm.sem, job_mm.at(row, SJ + 1))
            act.wait_ge(b_st.sem, b_st.at(row - 1, 16))
            act.activation(db[:], ring[0:48, (par + SJ) % 2, :], ACT.Identity, bias=b_db[:]).then_inc(job_ev.sem, 1)

        def u_bias(act, row, par, m):
            act.wait_ge(job_mm.sem, job_mm.at(row, UJ[m] + 1))
            act.wait_ge(ys_read.sem, ys_read.at(row - 2, ND))
            act.activation(u[:, par, m, :], ring[:, (par + UJ[m]) % 2, :], ACT.Identity,
                           bias=b_u[:, m:m + 1]).then_inc(job_ev.sem, 1)

        def step_size(act, row, par, m):
            act.wait_ge(job_mm.sem, job_mm.at(row, DJ + m + 1))
            act.activation(tail_of_xc[:, m, :], ring[:, (par + DJ + m) % 2, :], ACT.Abs)
            act.activation(delta[:, par, m, :], ring[:, (par + DJ + m) % 2, :], ACT.Relu).then_inc(job_ev.sem, 1)

        def exp_part(act, row):
            act.wait_ge(job_ev.sem, job_ev.at(row, DJ + ND))
            act.activation(tail_of_xc, tail_of_xc, ACT.Exp, scale=-1.0).then_inc(exp_done.sem, 1)

        def log_part(act, row):
            act.wait_ge(exp_done.sem, exp_done.at(row, 1))
            act.activation(tail_of_xc, tail_of_xc, ACT.Ln, bias=1.0).then_inc(log_done.sem, 1)

        def decay_step(act, row, par, s):
            g, dt, part = step_of(s)
            if g == 0 and part == 0:
                act.wait_ge(reset_ready.sem, reset_ready.at(row, dt + 1))
            act.wait_ge(scanned.sem, scanned.at(row, s + 1 - DEEP))
            for i in range(SN):
                ins = act.activation(da[:, s % DEEP, i, :], delta[:, par, dt, :], ACT.Exp,
                                     scale=-float(g * GN + part * SN + i + 1))
            ins.then_inc(da_ready.sem, 1)

        def conv_step(dve, row, m):
            dve.wait_ge(job_ev.sem, job_ev.at(row, IJ + m + 1))
            dve.wait_ge(job_mm.sem, job_mm.at(row - 1, UJ[-1] + 1))
            dve.tensor_scalar(hx[:, m, :], xc[:, m, 0:T], w_conv[:, m, 0:1], b_conv[:, m:m + 1],
                              ALU.mult, ALU.add).then_inc(conv.sem, 1)
            for t in range(1, DC):
                dve.wait_ge(conv.sem, conv.at(row, DC * m + t))
                dve.scalar_tensor_tensor(hx[:, m, :], xc[:, m, t:t + T], w_conv[:, m, t:t + 1], hx[:, m, :],
                                         ALU.mult, ALU.add).then_inc(conv.sem, 1)

        def silu_x(dve, row, m):
            dve.wait_ge(thx_ready.sem, thx_ready.at(row, m + 1))
            dve.scalar_tensor_tensor(hx[:, m, :], th[:, m % 2, :], 1.0, hx[:, m, :], ALU.add,
                                     ALU.mult).then_inc(xc_ready.sem, 1)

        def silu_z(dve, row, par, m):
            dve.wait_ge(thz_ready.sem, thz_ready.at(row, m + 1))
            dve.scalar_tensor_tensor(sz[:, par, m, :], th[:, m % 2, :], 1.0, sz[:, par, m, :], ALU.add,
                                     ALU.mult).then_inc(sz_ready.sem, 1)

        def softplus(dve, row, par, m):
            dve.wait_ge(log_done.sem, log_done.at(row, 1))
            dve.tensor_tensor(delta[:, par, m, :], delta[:, par, m, :], tail_of_xc[:, m, :],
                              ALU.add).then_inc(delta_ready.sem, 1)

        def step_input(dve, row, par, m):
            dve.wait_ge(delta_ready.sem, delta_ready.at(row, m + 1))
            dve.wait_ge(job_ev.sem, job_ev.at(row, UJ[m] + 1))
            dve.wait_ge(dbu_ready.sem, dbu_ready.at(row - 2, STEPS))
            dve.tensor_tensor(du[:, par, m, :], delta[:, par, m, :], u[:, par, m, :], ALU.mult).then_inc(du_ready.sem, 1)
            dve.wait_ge(du_ready.sem, du_ready.at(row, m + 1))
            dve.memset(delta[:, par, m, 0:1], RESET).then_inc(reset_ready.sem, 1)

        def scan_step(dve, row, s):
            dve.wait_ge(da_ready.sem, da_ready.at(row, s + 1))
            dve.wait_ge(dbu_ready.sem, dbu_ready.at(row, s + 1))
            dve.wait_ge(summed.sem, summed.at(row, s + 1 - DEEP))
            flat = [t[:, s % DEEP].rearrange("p n t -> p (n t)") for t in (hs, da, dbu)]
            dve.tensor_tensor_scan(flat[0], flat[1], flat[2], 0.0, ALU.mult, ALU.add).then_inc(scanned.sem, 1)

        def add_states(dve, row, s):
            dve.wait_ge(scanned.sem, scanned.at(row, s + 1))
            dve.tensor_tensor(hs[:, s % DEEP, 0, :], hs[:, s % DEEP, 0, :], hs[:, s % DEEP, 1, :],
                              ALU.add).then_inc(added.sem, 1)

        def gate(dve, row, par, dt):
            dve.wait_ge(summed.sem, summed.at(row, STEPS - STEPS // NG + (GN // SN) * (dt + 1)))
            dve.scalar_tensor_tensor(u[:, par, dt, :], u[:, par, dt, :], d_skip[:, dt:dt + 1], ys[:, dt, :], ALU.mult,
                                     ALU.add).then_inc(ys_read.sem, 1)
            dve.wait_ge(ys_read.sem, ys_read.at(row, dt + 1))
            dve.wait_ge(sz_ready.sem, sz_ready.at(row, dt + 1))
            dve.tensor_tensor(sz[:, par, dt, :], u[:, par, dt, :], sz[:, par, dt, :], ALU.mult).then_inc(y2_ready.sem, 1)

        def residual(dve, row, h):
            dve.wait_ge(o_mm.sem, o_mm.at(row, h + 1))
            dve.wait_ge(x1_based.sem, x1_based.at(row, 1))
            dve.tensor_tensor(x1[:, 2 * h:2 * h + 2, :], ob[:, h, :].rearrange("p (j c) -> p j c", c=C),
                              x1[:, 2 * h:2 * h + 2, :], ALU.add).then_inc(x1_ready.sem, 1)

        def route_stats(dve, row):
            dve.wait_ge(x1_ready.sem, x1_ready.at(row, 2))
            norm_stats(dve, r.norm, x1, row)

        def job_bank(pe, row, par, job):
            pe.wait_ge(job_ev.sem, job_ev.at(row, job - 1))
            return ring[:, (par + job) % 2, :]

        def turn(pe, row, par, c):
            bank = job_bank(pe, row, par, TJ + c)
            pe.wait_ge(norm.ready.sem, norm.ready.at(row, NT))
            for j in range(NT):
                mm = pe.transpose(bank[:, j * P:(j + 1) * P], xt[:, j, c * P:(c + 1) * P], k.ident[:])
            mm.then_inc(job_mm.sem, 1)

        def in_proj(pe, row, par, job, m):
            bank = job_bank(pe, row, par, job)
            pe.wait_ge(job_ev.sem, job_ev.at(row, TJ + NC))
            for c in range(NC):
                mm = pe.matmul(bank, w_in[:, c, m * P:(m + 1) * P], xnT[:, c, :], start=(c == 0), stop=(c == NC - 1))
            mm.then_inc(job_mm.sem, 1)

        def x_proj_small(pe, row, par, half):
            bank = job_bank(pe, row, par, SJ) if half == 0 else ring[:, (par + SJ) % 2, :]
            pe.wait_ge(xc_ready.sem, xc_ready.at(row, (half + 1) * ND // 2))
            for d in range(half * ND // 2, (half + 1) * ND // 2):
                mm = pe.matmul(bank[0:48, :], w_x[:, d, DI:], hx[:, d, :], start=(d == 0), stop=(d == ND - 1))
            if half == 1:
                mm.then_inc(job_mm.sem, 1)

        def x_proj(pe, row, par, m, half):
            bank = job_bank(pe, row, par, UJ[m]) if half == 0 else ring[:, (par + UJ[m]) % 2, :]
            for d in range(half * ND // 2, (half + 1) * ND // 2):
                mm = pe.matmul(bank, w_x[:, d, m * P:(m + 1) * P], hx[:, d, :], start=(d == 0), stop=(d == ND - 1))
            if half == 1:
                mm.then_inc(job_mm.sem, 1)

        def dt_proj(pe, row, par, m):
            bank = job_bank(pe, row, par, DJ + m)
            pe.wait_ge(job_ev.sem, job_ev.at(row, SJ + 1))
            pe.matmul(bank, w_dt[:, m * P:(m + 1) * P], db[0:32, :], start=True, stop=True).then_inc(job_mm.sem, 1)

        def sum_step(pe, row, s):
            g, dt, part = step_of(s)
            if s in ADDED:
                pe.wait_ge(added.sem, added.at(row, ADDED.index(s) + 1))
            else:
                pe.wait_ge(scanned.sem, scanned.at(row, s + 1))
            if g == 0 and part == 0:
                pe.wait_ge(ys_read.sem, ys_read.at(row - 1, dt + 1))
            terms = 1 if s in ADDED else SN
            for i in range(terms):
                mm = pe.matmul(ys[:, dt, :], k.ident[:], hs[:, s % DEEP, i, :], start=(g == 0 and part == 0 and i == 0),
                               stop=(g == NG - 1 and part == GN // SN - 1 and i == terms - 1))
            mm.then_inc(summed.sem, 1)

        def out_proj(pe, row, par, j):
            if j == 0:
                pe.wait_ge(y2_ready.sem, y2_ready.at(row, ND))
                pe.wait_ge(r.done.sem, r.done.at(row - 1, 1))
            h, q = j // 2, j % 2
            for d in range(ND):
                mm = pe.matmul(ob[:, h, q * C:(q + 1) * C], sz[:, par, d, j * P:(j + 1) * P], w_out[:, d, :],
                               start=(d == 0), stop=(d == ND - 1))
            if q == 1:
                mm.then_inc(o_mm.sem, 1)

        def rows(eng, one_row):
            one_row(0, 0)
            one_row(1, 1)
            with eng.Fori(1, B // 2 - 1) as pair:
                one_row(2 * pair, 0)
                one_row(2 * pair + 1, 1)
            one_row(B - 2, 0)
            one_row(B - 1, 1)

        def is_row(row, n):
            return isinstance(row, int) and row == n

        def last(row):
            return is_row(row, B - 1)

        def first(row):
            return is_row(row, 0)

        with nc.Block() as block:
            @block.sync
            def _(sp):
                load_x(sp, 0)
                load_consts(sp)
                load_x(sp, 1)
                store_b(sp, 0, 0)
                spread_b(sp, 0, 0, 0)

                def one_row(row, par):
                    spread_b(sp, row, par, 1)
                    if not (last(row) or is_row(row, B - 2)):
                        load_x(sp, row + 2)
                    spread_b(sp, row, par, 2)
                    if not first(row):
                        store_x1(sp, row - 1)
                    load_x1(sp, row)
                    spread_b(sp, row, par, 3)
                    if not last(row):
                        store_b(sp, row + 1, 1 - par)
                        spread_b(sp, row + 1, 1 - par, 0)

                rows(sp, one_row)
                store_x1(sp, B - 1)
                sp.wait_ge(x1_st.sem, x1_st.at(B - 1, 16))

            @block.gpsimd
            def _(pool):
                pool.memset(w_dt[:], 0.0).then_inc(dt_cleared, 1)
                pool.memset(b_db[:], 0.0).then_inc(bias_one, 1)
                pool.wait_ge(bias_one, 1)
                pool.affine_select(out=b_db[:], in_=b_db[:], compare_op=ALU.not_equal, fill=1.0, base=-NS,
                                   pattern=[[0, 1]], channel_multiplier=1).then_inc(bias_one, 1)
                pool.memset(w_x[:, :, DI + NS:DI + 32], 0.0).then_inc(cleared, 1)
                pool.memset(xc[:, :, 0:DC - 1], 0.0).then_inc(cleared, 1)
                pool.wait_ge(loaded, 16 * CONSTS)
                norm_rstd(pool, norm, 0)

                def one_row(row, par):
                    for s in range(STEPS):
                        input_step(pool, row, par, s)
                        if s == 4 and not last(row):
                            norm_rstd(pool, norm, row + 1)
                        if s == 20 and not first(row):
                            norm_rstd(pool, r.norm, row - 1)
                        if s == 22:
                            add_out_bias(pool, row)
                        if 1 <= s < 1 + NT * K and not (first(row) or is_row(row, 1)):
                            route_send(pool, r, row - 2, s - 1)

                rows(pool, one_row)
                for n in range(NT * K):
                    route_send(pool, r, B - 2, n)
                norm_rstd(pool, r.norm, B - 1)
                for n in range(NT * K):
                    route_send(pool, r, B - 1, n)
                pool.wait_ge(r.sent.sem, r.sent.at(B - 1, 16 * NT * K))

            @block.scalar
            def _(act):
                act.wait_ge(loaded, 16 * CONSTS)
                act.wait_ge(halved, 3)

                def first_part(row, par, s):
                    if s == 8:
                        for c in range(NC):
                            turned(act, row, par, c)
                    for m in range(ND):
                        if s == 9 + m:
                            conv_input(act, row, par, m)
                        if s == (12, 14, 16, 17)[m]:
                            tanh_x(act, row, m)
                    if s == 20:
                        delta_b(act, row, par)
                    if s == 22:
                        u_bias(act, row, par, 0)
                    if s in (23, 24):
                        for m in range((s - 23) * 2, (s - 22) * 2):
                            step_size(act, row, par, m)
                    if s == 25:
                        exp_part(act, row)
                    if s == 26:
                        log_part(act, row)
                    if s in (27, 30):
                        u_bias(act, row, par, s // 3 - 8)

                for s in range(STEPS):
                    first_part(0, 0, s)

                def one_row(row, par):
                    for s in range(STEPS):
                        decay_step(act, row, par, s)
                        if s == 0:
                            u_bias(act, row, par, ND - 1)
                        if 4 <= s < 4 + ND:
                            gate_input(act, row, par, s - 4)
                        if 8 <= s < 8 + ND:
                            tanh_z(act, row, par, s - 8)
                        if not last(row):
                            first_part(row + 1, 1 - par, s)
                        if not first(row):
                            if s == 24:
                                for c in range(NC):
                                    route_turned(act, r, row - 1, c)
                            if s == 30:
                                route_exp(act, r, row - 1)

                rows(act, one_row)
                for c in range(NC):
                    route_turned(act, r, B - 1, c)
                route_exp(act, r, B - 1)

            @block.vector
            def _(dve):
                dve.wait_ge(loaded, 16 * CONSTS)
                dve.wait_ge(cleared, 2)
                dve.tensor_scalar(b_z[:], b_in[:, ND:], 0.5, None, ALU.mult).then_inc(halved, 1)
                dve.tensor_scalar(w_conv[:], w_conv[:], 0.5, None, ALU.mult).then_inc(halved, 1)
                dve.tensor_scalar(b_conv[:], b_conv[:], 0.5, None, ALU.mult).then_inc(halved, 1)
                dve.wait_ge(halved, 3)

                def first_part(row, par, s):
                    if s == 0:
                        dve.wait_ge(x_ld.sem, x_ld.at(row, 16))
                        norm_stats(dve, norm, xt, row)
                    if s == 3:
                        norm_apply(dve, norm, xt, xt, row)
                    for m in range(ND):
                        if s == (8, 10, 12, 13)[m]:
                            conv_step(dve, row, m)
                        if s == (10, 12, 14, 15)[m]:
                            silu_x(dve, row, m)
                        if s == 24 + m // 2:
                            softplus(dve, row, par, m)
                        if m < ND - 1 and s == 25 + 2 * m:
                            step_input(dve, row, par, m)

                for s in range(STEPS):
                    first_part(0, 0, s)

                def one_row(row, par):
                    for s in range(STEPS):
                        scan_step(dve, row, s)
                        if s - 1 in ADDED:
                            add_states(dve, row, s - 1)
                        if s == 1:
                            step_input(dve, row, par, ND - 1)
                        for m in range(ND):
                            if s == (6, 7, 9, 11)[m]:
                                silu_z(dve, row, par, m)
                        if not first(row):
                            if s in (2, 4):
                                gate(dve, row - 1, 1 - par, ND - 3 + s // 2)
                            if s in (13, 15):
                                residual(dve, row - 1, (s - 13) // 2)
                            if s == 16:
                                route_stats(dve, row - 1)
                            if s == 19:
                                route_norm(dve, r, x1, row - 1)
                            if s == 26:
                                route_best(dve, r, row - 1)
                            if s == 29:
                                route_slots(dve, r, row - 1)
                        if not last(row):
                            first_part(row + 1, 1 - par, s)
                        if s in (28, 30):
                            gate(dve, row, par, (s - 28) // 2)

                rows(dve, one_row)
                for dt in (ND - 2, ND - 1):
                    gate(dve, B - 1, 1, dt)
                for h in range(2):
                    residual(dve, B - 1, h)
                route_stats(dve, B - 1)
                route_norm(dve, r, x1, B - 1)
                route_best(dve, r, B - 1)
                route_slots(dve, r, B - 1)

            @block.tensor
            def _(pe):
                pe.wait_ge(loaded, 16 * CONSTS)
                pe.wait_ge(cleared, 1)

                def first_part(row, par, s):
                    if s == 4:
                        for c in range(NC):
                            turn(pe, row, par, c)
                    if 5 <= s < 5 + ND:
                        in_proj(pe, row, par, IJ + s - 5, s - 5)
                    if s in (15, 16):
                        x_proj_small(pe, row, par, s - 15)
                    if s in (17, 18):
                        x_proj(pe, row, par, 0, s - 17)
                    if s in (19, 20):
                        for m in range((s - 19) * 2, (s - 18) * 2):
                            dt_proj(pe, row, par, m)
                    for m in range(1, ND):
                        if s in (19 + 3 * m, 20 + 3 * m):
                            x_proj(pe, row, par, m, s - 19 - 3 * m)

                for s in range(STEPS):
                    first_part(0, 0, s)

                def one_row(row, par):
                    for s in range(STEPS):
                        sum_step(pe, row, s)
                        if s < ND:
                            in_proj(pe, row, par, ZJ + s, ND + s)
                        if not first(row):
                            for j in range(NT):
                                if s == (9, 11, 12, 13)[j]:
                                    out_proj(pe, row - 1, 1 - par, j)
                            if s == 21:
                                for c in range(NC):
                                    route_transpose(pe, r, row - 1, c)
                            if s == 24:
                                route_logits(pe, r, row - 1)
                            if s == 27:
                                route_places(pe, r, row - 1)
                        if not last(row):
                            first_part(row + 1, 1 - par, s)

                rows(pe, one_row)
                for j in range(NT):
                    out_proj(pe, B - 1, 1, j)
                for c in range(NC):
                    route_transpose(pe, r, B - 1, c)
                route_logits(pe, r, B - 1)
                route_places(pe, r, B - 1)


class Mixer:

    def __init__(self, sb, sem, name, k, copies, ahead, first=0):
        self.k, self.copies, self.first = k, copies, first
        self.index = sb(name + "_index", [P, copies, NT * K], U32)
        self.got, self.share = sb(name + "_got", [P, copies, NT * K, C]), sb(name + "_share", [P, NT * K])
        self.index_ready = Count(sem(name + "_index_ready"), 1)
        self.pool_held = sem(name + "_pool_held")
        self.fetched = [Count(sem(f"{name}_fetched{i}"), 16 * NT * K) for i in range(copies)]
        self.steps = Count(sem(name + "_steps"), 1 + NT * K, ahead)


def mix_fetch(pool, x, row, nth, copy):
    turn = row - x.first
    pool.wait_ge(x.steps.sem, x.steps.at(turn - x.copies, 1 + NT * K))
    pool.tensor_copy(x.index[:, copy, :], x.k.fetch[:, bass.ds(row, 1), :].rearrange("p a s -> p (a s)")) \
        .then_inc(x.index_ready.sem, 1)
    pool.wait_ge(x.index_ready.sem, x.index_ready.at(turn, 1))
    pool.sem_inc(x.pool_held, 1)
    for s in range(NT * K):
        pool.indirect_dma_start(x.got[:, copy, s, :], None, x.k.results,
                                bass.IndirectOffsetOnAxis(ap=x.index[:, copy, s:s + 1], axis=0),
                                bounds_check=SLOTS - 1, oob_is_err=False).then_inc(x.fetched[copy].sem, 16)


def mix(dve, x, row, nth, copy, base, out):
    done, turn = x.steps, row - x.first
    dve.tensor_copy(x.share[:], x.k.share[:, bass.ds(row, 1), :].rearrange("p a s -> p (a s)")).then_inc(done.sem, 1)
    dve.wait_ge(x.fetched[copy].sem, x.fetched[copy].at(nth, 16 * NT * K))
    for kk in range(K):
        dve.wait_ge(done.sem, done.at(turn, 1 + kk * NT))
        for j in range(NT):
            at = j * K + kk
            dve.scalar_tensor_tensor(out[:, j, :], x.got[:, copy, at, :], x.share[:, at:at + 1],
                                     (base if kk == 0 else out)[:, j, :], ALU.mult, ALU.add).then_inc(done.sem, 1)
    dve.wait_ge(done.sem, done.at(turn, 1 + NT * K))


def experts_phase(nc, k, w, name, out=None):
    with ExitStack() as ctx:
        def sb(n, shape, dt=F32):
            return ctx.enter_context(nc.sbuf_tensor(f"{name}_{n}", shape, dt))

        def sem(n):
            return ctx.enter_context(nc.semaphore(f"{name}_{n}"))

        TURNS = 2 * E
        HN = 2
        HW = ROWS // HN
        TJ = 3
        WP = 4
        HB = 4

        w1, w2 = sb("w1", [P, NC, H]), sb("w2", [P, NH, C])
        w1_hi, w1_lo = (sb(n, [P, 2, NC, H], F32R) for n in ("w1_hi", "w1_lo"))
        w2_hi, w2_lo = (sb(n, [P, 2, NH, C], F32R) for n in ("w2_hi", "w2_lo"))
        b1, b2 = sb("b1", [P, 2, NH]), sb("b2", [P, 2, C])
        rows = sb("rows", [P, 2, NR, C])
        rowsT_hi, rowsT_lo = (sb(n, [P, NC, ROWS], F32R) for n in ("rowsT_hi", "rowsT_lo"))
        h = sb("h", [P, HB, ROWS])
        hT_hi, hT_lo = (sb(n, [P, NH, ROWS], F32R) for n in ("hT_hi", "hT_lo"))
        y = sb("y", [P, 2, NR, C])
        tbank = ctx.enter_context(nc.psum_tensor(name + "_tbank", [P, 2, 512], F32))
        hbank = ctx.enter_context(nc.psum_tensor(name + "_hbank", [P, 4, 512], F32))
        ybank = ctx.enter_context(nc.psum_tensor(name + "_ybank", [P, 2, 512], F32))

        if out is not None:
            xa, xo = sb("xa", [P, 2, NT, C]), sb("xo", [P, 2, NT, C])
            mixer = Mixer(sb, sem, "mix", k, 1, 1)
            x_ld = [Count(sem(f"x_ld{i}"), 16) for i in range(2)]
            xo_st, xo_free = Count(sem("xo_st"), 16), Count(sem("xo_free"), 1, ahead=2)

        w_loaded = Count(sem("w_loaded"), 32)
        loaded = [Count(sem(f"loaded{i}"), 32) for i in range(2)]
        w_hi, w_lo = Count(sem("w_hi"), 2 * WP), Count(sem("w_lo"), 2 * WP, ahead=1)
        stored, y_free = Count(sem("stored"), 16), Count(sem("y_free"), 1, ahead=2)
        b1_ready = Count(sem("b1_ready"), 1)
        t_mm, t_hi, t_lo = Count(sem("t_mm"), TJ), Count(sem("t_hi"), TJ), Count(sem("t_lo"), TJ, ahead=1)
        h_mm, h_ev = Count(sem("h_mm"), NH * HN), Count(sem("h_ev"), NH * HN, ahead=1)
        h_hi, h_lo = Count(sem("h_hi"), NH), Count(sem("h_lo"), NH, ahead=1)
        y_mm, y_ev = Count(sem("y_mm"), NR, ahead=2), Count(sem("y_ev"), NR, ahead=2)

        def load(sp, turn, par, e):
            sp.wait_ge(w_lo.sem, w_lo.at(turn - 1, 2 * WP))
            for dst, src in ((w1[:], w["W1"][e].rearrange("(k p) h -> p k h", p=P)),
                             (w2[:], w["W2"][e].rearrange("(m p) c -> p m c", p=P))):
                sp.dma_start(dst, src).then_inc(w_loaded.sem, 16)
            sp.wait_ge(y_ev.sem, y_ev.at(turn - 2, NR))
            for dst, src in ((rows[:, par], k.slots[bass.ds(turn * ROWS, ROWS)].rearrange("(r p) c -> p r c", p=P)),
                             (b2[:, par], w["b2"][e].partition_broadcast(P))):
                sp.dma_start(dst, src).then_inc(loaded[par].sem, 16)

        def weight_piece(piece, par):
            if piece < WP:
                c, at = piece // (WP // NC), slice(piece % (WP // NC) * (H * NC // WP), (piece % (WP // NC) + 1) * (H * NC // WP))
                return w1[:, c, at], w1_hi[:, par, c, at], w1_lo[:, par, c, at]
            at = slice((piece - WP) * (NH // WP), (piece - WP + 1) * (NH // WP))
            return w2[:, at], w2_hi[:, par, at], w2_lo[:, par, at]

        def weight_high(act, turn, par, piece):
            act.wait_ge(w_loaded.sem, w_loaded.at(turn, 32))
            act.wait_ge(y_mm.sem, y_mm.at(turn - 2, NR))
            full, high, low = weight_piece(piece, par)
            act.activation(high, full, ACT.Copy).then_inc(w_hi.sem, 1)

        def weight_low(pool, turn, par, piece):
            pool.wait_ge(w_hi.sem, w_hi.at(turn, piece + 1))
            full, high, low = weight_piece(piece, par)
            pool.tensor_tensor(low, full, high.bitcast(F32), ALU.subtract).then_inc(w_lo.sem, 1)

        def turn_rows(pe, turn, pair, par):
            pe.wait_ge(loaded[par].sem, loaded[par].at(pair, 32))
            for job in range(TJ):
                if job < 2:
                    pe.wait_ge(t_lo.sem, t_lo.at(turn - 1, TJ - job))
                    for r in range(4):
                        mm = pe.transpose(tbank[:, job, r * P:(r + 1) * P], rows[:, par, r, job * P:(job + 1) * P],
                                          k.ident[:])
                else:
                    pe.wait_ge(t_lo.sem, t_lo.at(turn, 1))
                    for c in range(NC):
                        mm = pe.transpose(tbank[:, 0, c * P:(c + 1) * P], rows[:, par, 4, c * P:(c + 1) * P], k.ident[:])
                mm.then_inc(t_mm.sem, 1)

        def turned_part(t, job):
            if job < 2:
                return t[:, job, 0:512], tbank[:, job, :]
            return t[:, :, 512:ROWS], tbank[:, 0, 0:NC * P].rearrange("p (c t) -> p c t", t=P)

        def turned_high(act, turn):
            for job in range(TJ):
                act.wait_ge(t_mm.sem, t_mm.at(turn, job + 1))
                high, bank = turned_part(rowsT_hi, job)
                act.activation(high, bank, ACT.Copy).then_inc(t_hi.sem, 1)

        def turned_low(dve, turn):
            for job in range(TJ):
                dve.wait_ge(t_hi.sem, t_hi.at(turn, job + 1))
                high, bank = turned_part(rowsT_hi, job)
                low, bank = turned_part(rowsT_lo, job)
                dve.tensor_tensor(low, bank, high.bitcast(F32), ALU.subtract).then_inc(t_lo.sem, 1)

        def first_product(pe, turn, par):
            for m in range(NH):
                for n in range(HN):
                    job = m * HN + n
                    if job == 0:
                        pe.wait_ge(t_lo.sem, t_lo.at(turn, TJ))
                        pe.wait_ge(w_lo.sem, w_lo.at(turn, 2 * WP))
                    pe.wait_ge(h_ev.sem, h_ev.at(turn, job - 3))
                    for c in range(NC):
                        ws, rs = slice(m * P, (m + 1) * P), slice(n * HW, (n + 1) * HW)
                        pe.matmul(hbank[:, job % 4, 0:HW], w1_hi[:, par, c, ws], rowsT_hi[:, c, rs], start=(c == 0), stop=False)
                        pe.matmul(hbank[:, job % 4, 0:HW], w1_hi[:, par, c, ws], rowsT_lo[:, c, rs], start=False, stop=False)
                        mm = pe.matmul(hbank[:, job % 4, 0:HW], w1_lo[:, par, c, ws], rowsT_hi[:, c, rs], start=False,
                                       stop=(c == NC - 1))
                    mm.then_inc(h_mm.sem, 1)

        def relu(act, turn, par, m):
            for n in range(HN):
                job = m * HN + n
                act.wait_ge(h_lo.sem, h_lo.at(turn, m + 1 - HB))
                act.wait_ge(h_mm.sem, h_mm.at(turn, job + 1))
                act.activation(h[:, m % HB, n * HW:(n + 1) * HW], hbank[:, job % 4, 0:HW], ACT.Relu,
                               bias=b1[:, par, m:m + 1]).then_inc(h_ev.sem, 1)

        def split_hidden(dve, turn, m):
            dve.wait_ge(h_ev.sem, h_ev.at(turn, (m + 1) * HN))
            dve.tensor_copy(hT_hi[:, m, :], h[:, m % HB, :]).then_inc(h_hi.sem, 1)
            dve.wait_ge(h_hi.sem, h_hi.at(turn, m + 1))
            dve.tensor_tensor(hT_lo[:, m, :], h[:, m % HB, :], hT_hi[:, m, :].bitcast(F32),
                              ALU.subtract).then_inc(h_lo.sem, 1)

        def second_product(pe, turn, par):
            for r in range(NR):
                pe.wait_ge(y_ev.sem, y_ev.at(turn, r - 1))
                for m in range(NH):
                    if r == 0:
                        pe.wait_ge(h_lo.sem, h_lo.at(turn, m + 1))
                    bank, rs = ybank[:, (par + r) % 2, 0:C], slice(r * P, (r + 1) * P)
                    pe.matmul(bank, hT_hi[:, m, rs], w2_hi[:, par, m, :], start=(m == 0), stop=False)
                    pe.matmul(bank, hT_hi[:, m, rs], w2_lo[:, par, m, :], start=False, stop=False)
                    mm = pe.matmul(bank, hT_lo[:, m, rs], w2_hi[:, par, m, :], start=False, stop=(m == NH - 1))
                mm.then_inc(y_mm.sem, 1)

        def second_bias(dve, turn, par):
            dve.wait_ge(y_free.sem, y_free.at(turn - 2, 1))
            for r in range(NR):
                dve.wait_ge(y_mm.sem, y_mm.at(turn, r + 1))
                dve.tensor_tensor(y[:, par, r, :], ybank[:, (par + r) % 2, 0:C], b2[:, par, :],
                                  ALU.add).then_inc(y_ev.sem, 1)

        def store(pool, turn, par):
            pool.wait_ge(y_ev.sem, y_ev.at(turn, NR))
            pool.dma_start(k.results[bass.ds(turn * ROWS, ROWS)].rearrange("(r p) c -> p r c", p=P),
                           y[:, par]).then_inc(stored.sem, 16)
            pool.wait_ge(stored.sem, stored.at(turn, 16))
            pool.sem_inc(y_free.sem, 1)

        def load_x(sp, row, nth, par):
            sp.wait_ge(mixer.steps.sem, mixer.steps.at(row - 2, 1 + NT * K))
            sp.dma_start(xa[:, par], k.x3[bass.ds(row, 1)].rearrange("a (j p) c -> p (a j) c", p=P)).then_inc(x_ld[par].sem, 16)

        def mix_row(dve, row, nth, par):
            dve.wait_ge(x_ld[par].sem, x_ld[par].at(nth, 16))
            dve.wait_ge(xo_free.sem, xo_free.at(row - 2, 1))
            mix(dve, mixer, row, row, 0, xa[:, par], xo[:, par])

        def store_row(pool, row, par):
            pool.wait_ge(mixer.steps.sem, mixer.steps.at(row, 1 + NT * K))
            pool.dma_start(out[bass.ds(row, 1)].rearrange("a (j p) c -> p (a j) c", p=P), xo[:, par]).then_inc(xo_st.sem, 16)
            pool.wait_ge(xo_st.sem, xo_st.at(row, 16))
            pool.sem_inc(xo_free.sem, 1)

        def turns(eng, one_turn):
            with eng.Fori(0, E // 2) as pair:
                one_turn(2 * pair, pair, 0, None)
                one_turn(2 * pair + 1, pair + 1, 1, None)
            with eng.Fori(E // 2, E - 1) as pair:
                one_turn(2 * pair, pair, 0, 2 * pair - E)
                one_turn(2 * pair + 1, pair + 1, 1, 2 * pair + 1 - E)
            one_turn(TURNS - 2, E - 1, 0, HALF - 2)
            one_turn(TURNS - 1, E, 1, HALF - 1)

        def last(turn):
            return isinstance(turn, int) and turn == TURNS - 1

        def mixes(row):
            return out is not None and row is not None

        with nc.Block() as block:
            @block.sync
            def _(sp):
                with sp.Fori(0, E // 2) as pair:
                    for par in range(2):
                        load(sp, pair * 2 + par, par, pair * 2 + par)
                with sp.Fori(0, E // 2) as pair:
                    for par in range(2):
                        load(sp, E + pair * 2 + par, par, pair * 2 + par)
                        if mixes(pair):
                            load_x(sp, pair * 2 + par, pair, par)

            @block.tensor
            def _(pe):
                y_mm.grant(pe)
                turn_rows(pe, 0, 0, 0)

                def one_turn(turn, next_pair, par, row):
                    first_product(pe, turn, par)
                    if not last(turn):
                        turn_rows(pe, turn + 1, next_pair, 1 - par)
                    second_product(pe, turn, par)

                turns(pe, one_turn)

            @block.scalar
            def _(act):
                h_ev.grant(act)
                for piece in range(2 * WP):
                    weight_high(act, 0, 0, piece)
                turned_high(act, 0)

                def one_turn(turn, next_pair, par, row):
                    act.activation(b1[:, par, :], k.b1[:, bass.ds(turn, 1), :].rearrange("p a m -> p (a m)"),
                                   ACT.Copy).then_inc(b1_ready.sem, 1)
                    act.wait_ge(b1_ready.sem, b1_ready.at(turn, 1))
                    for m in range(NH):
                        relu(act, turn, par, m)
                        if not last(turn):
                            weight_high(act, turn + 1, 1 - par, m)
                    if not last(turn):
                        turned_high(act, turn + 1)

                turns(act, one_turn)

            @block.vector
            def _(dve):
                t_lo.grant(dve)
                h_lo.grant(dve)
                y_ev.grant(dve)
                if out is not None:
                    mixer.steps.grant(dve)
                turned_low(dve, 0)

                def one_turn(turn, next_pair, par, row):
                    for m in range(NH):
                        split_hidden(dve, turn, m)
                    if not last(turn):
                        turned_low(dve, turn + 1)
                    second_bias(dve, turn, par)
                    if mixes(row):
                        mix_row(dve, row, next_pair - E // 2 - par, par)

                turns(dve, one_turn)

            @block.gpsimd
            def _(pool):
                w_lo.grant(pool)
                y_free.grant(pool)
                if out is not None:
                    xo_free.grant(pool)
                for piece in range(2 * WP):
                    weight_low(pool, 0, 0, piece)

                def one_turn(turn, next_pair, par, row):
                    if not last(turn):
                        for piece in range(2 * WP):
                            weight_low(pool, turn + 1, 1 - par, piece)
                    if mixes(row):
                        mix_fetch(pool, mixer, row, row, 0)
                    store(pool, turn, par)
                    if mixes(row):
                        store_row(pool, row, par)

                turns(pool, one_turn)
                pool.wait_ge(stored.sem, stored.at(TURNS - 1, 16))


def attention_phase(nc, k, w):
    with ExitStack() as ctx:
        def sb(name, shape, dt=F32):
            return ctx.enter_context(nc.sbuf_tensor("a_" + name, shape, dt))

        def sem(name):
            return ctx.enter_context(nc.semaphore("a_" + name))

        GAMMA = 1.0 / float(np.sqrt(np.float32(C)))
        wq, wk, wv = (sb(n, [P, NC, C]) for n in ("wq", "wk", "wv"))
        xa, x2 = sb("xa", [P, NT, C]), sb("x2", [P, 2, NT, C])
        xn, xnT = sb("xn", [P, NT, C]), sb("xnT", [P, NC, T])
        qT, kT, v = sb("qT", [P, NC, T]), sb("kT", [P, NC, T]), sb("v", [P, NT, C])
        top, bias = sb("top", [P, NT]), sb("bias", [P, NT])
        pr, prT = sb("pr", [P, 2, T]), sb("prT", [P, 2, T])
        total, inverse = sb("total", [P, NT]), sb("inverse", [P, NT])
        x3 = sb("x3", [P, NT, C])
        ring = ctx.enter_context(nc.psum_tensor("a_ring", [P, 2, T], F32))
        sbank = ctx.enter_context(nc.psum_tensor("a_sbank", [P, 2, T], F32))
        tbank = ctx.enter_context(nc.psum_tensor("a_tbank", [P, 2, T], F32))
        obank = ctx.enter_context(nc.psum_tensor("a_obank", [P, 2, T], F32))

        r = Router(sb, sem, k, [ring[:, 0, :], ring[:, 1, :]], ring[:, 0, :], ring[:, 0, P:])
        mixer = Mixer(sb, sem, "mix", k, 1, 0)
        norm = Norm(sb, sem, k, "norm")
        loaded = sem("loaded")
        x_ld, x3_st = Count(sem("x_ld"), 16), Count(sem("x3_st"), 16)
        t_mm, t_ev = Count(sem("t_mm"), NC), Count(sem("t_ev"), NC)
        QKV = 6
        qkv_mm, qkv_ev = Count(sem("qkv_mm"), QKV), Count(sem("qkv_ev"), QKV)
        s_mm, max_ready, exp_ready = Count(sem("s_mm"), NT), Count(sem("max_ready"), 2 * NT), Count(sem("exp_ready"), NT)
        p_mm, p_ev = Count(sem("p_mm"), NT), Count(sem("p_ev"), NT)
        o_mm, inv_ready, x3_ready = Count(sem("o_mm"), NT), Count(sem("inv_ready"), NT), Count(sem("x3_ready"), NT)

        def load_x(sp, row):
            sp.wait_ge(mixer.steps.sem, mixer.steps.at(row - 1, 1 + NT * K))
            sp.dma_start(xa[:], k.x1[row].rearrange("(j p) c -> p j c", p=P)).then_inc(x_ld.sem, 16)

        def store_x3(sp, row):
            sp.wait_ge(x3_ready.sem, x3_ready.at(row, NT))
            sp.dma_start(k.x3[row].rearrange("(j p) c -> p j c", p=P), x3[:]).then_inc(x3_st.sem, 16)

        def add_ffn(dve, row, par):
            dve.wait_ge(x_ld.sem, x_ld.at(row, 16))
            mix(dve, mixer, row, row, 0, xa, x2[:, par])

        def row_max(dve, row, i):
            dve.wait_ge(s_mm.sem, s_mm.at(row, i + 1))
            dve.tensor_reduce(top[:, i:i + 1], sbank[:, i % 2, 0:(i + 1) * P], AX.X, ALU.max).then_inc(max_ready.sem, 1)
            dve.wait_ge(max_ready.sem, max_ready.at(row, 2 * i + 1))
            dve.tensor_scalar(bias[:, i:i + 1], top[:, i:i + 1], -GAMMA, None, ALU.mult).then_inc(max_ready.sem, 1)

        def add_attention(dve, row, par, i):
            dve.wait_ge(exp_ready.sem, exp_ready.at(row, i + 1))
            dve.reciprocal(inverse[:, i:i + 1], total[:, i:i + 1]).then_inc(inv_ready.sem, 1)
            dve.wait_ge(inv_ready.sem, inv_ready.at(row, i + 1))
            dve.wait_ge(x3_st.sem, x3_st.at(row - 1, 16))
            dve.wait_ge(o_mm.sem, o_mm.at(row, i + 1))
            dve.scalar_tensor_tensor(x3[:, i, :], obank[:, i % 2, 0:C], inverse[:, i:i + 1], x2[:, par, i, :],
                                     ALU.mult, ALU.add).then_inc(x3_ready.sem, 1)

        def probs_turned(act, row, i):
            act.wait_ge(p_mm.sem, p_mm.at(row, i + 1))
            if i < 2:
                act.wait_ge(o_mm.sem, o_mm.at(row - 1, i + 3))
            else:
                act.wait_ge(o_mm.sem, o_mm.at(row, i - 1))
            act.activation(prT[:, i % 2, 0:(i + 1) * P], tbank[:, i % 2, 0:(i + 1) * P], ACT.Copy).then_inc(p_ev.sem, 1)

        def qkv_copy(act, row, job):
            act.wait_ge(qkv_mm.sem, qkv_mm.at(row, job + 1))
            dst = (qT[:, job, :] if job < NC else kT[:, job - NC, :] if job < 2 * NC
                   else v[:, 2 * (job - 2 * NC):2 * (job - 2 * NC) + 2, :].rearrange("p j c -> p (j c)"))
            act.activation(dst, ring[:, bank_of(job), :], ACT.Copy).then_inc(qkv_ev.sem, 1)

        def turned(act, row, c):
            act.wait_ge(t_mm.sem, t_mm.at(row, c + 1))
            act.activation(xnT[:, c, :], ring[:, c, :], ACT.Copy).then_inc(t_ev.sem, 1)

        def probs(act, row, i):
            act.wait_ge(max_ready.sem, max_ready.at(row, 2 * (i + 1)))
            if i < 2:
                act.wait_ge(p_mm.sem, p_mm.at(row - 1, i + 3))
            else:
                act.wait_ge(p_mm.sem, p_mm.at(row, i - 1))
            act.wait_ge(x3_ready.sem, x3_ready.at(row - 1, NT))
            act.activation(pr[:, i % 2, 0:(i + 1) * P], sbank[:, i % 2, 0:(i + 1) * P], ACT.Exp, bias=bias[:, i:i + 1],
                           scale=GAMMA, accum_out=total[:, i:i + 1]).then_inc(exp_ready.sem, 1)

        def bank_of(job):
            return job % 2 if job < 2 * NC else 1

        def qkv(pe, row, job):
            if job < 2:
                pe.wait_ge(t_ev.sem, t_ev.at(row, NC))
            else:
                pe.wait_ge(qkv_ev.sem, qkv_ev.at(row, job if job > 2 * NC else job - 1))
            if job == 2 * NC:
                pe.wait_ge(qkv_ev.sem, qkv_ev.at(row, job))
                pe.wait_ge(r.x_ev.sem, r.x_ev.at(row - 1, NC))
            if job < 2 * NC:
                wt, m = (wq, wk)[job // NC], job % NC
                for c in range(NC):
                    mm = pe.matmul(ring[:, bank_of(job), :], wt[:, c, m * P:(m + 1) * P], xnT[:, c, :], start=(c == 0),
                                   stop=(c == NC - 1))
            else:
                for q in range(2):
                    j = 2 * (job - 2 * NC) + q
                    for c in range(NC):
                        mm = pe.matmul(ring[:, bank_of(job), q * C:(q + 1) * C], xnT[:, c, j * P:(j + 1) * P], wv[:, c, :],
                                       start=(c == 0), stop=(c == NC - 1))
            mm.then_inc(qkv_mm.sem, 1)

        def scores(pe, row, i):
            if i == 0:
                pe.wait_ge(qkv_ev.sem, qkv_ev.at(row, 2 * NC))
            if i < 2:
                pe.wait_ge(exp_ready.sem, exp_ready.at(row - 1, i + 3))
            else:
                pe.wait_ge(exp_ready.sem, exp_ready.at(row, i - 1))
            bank = sbank[:, i % 2, :]
            pe.matmul(bank[:, 0:(i + 1) * P], k.identb[:], k.future[:, T - (i + 1) * P:], start=True, stop=False)
            for c in range(NC):
                mm = pe.matmul(bank[:, 0:(i + 1) * P], qT[:, c, i * P:(i + 1) * P], kT[:, c, 0:(i + 1) * P], start=False,
                               stop=(c == NC - 1))
            mm.then_inc(s_mm.sem, 1)

        def turn(pe, row, c):
            pe.wait_ge(norm.ready.sem, norm.ready.at(row, NT))
            pe.wait_ge(qkv_ev.sem, qkv_ev.at(row - 1, QKV))
            if c == 0:
                pe.wait_ge(r.steps.sem, r.steps.at(row - 2, PLACES))
            for j in range(NT):
                mm = pe.transpose(ring[:, c, j * P:(j + 1) * P], xn[:, j, c * P:(c + 1) * P], k.ident[:])
            mm.then_inc(t_mm.sem, 1)

        def turn_probs(pe, row, i):
            pe.wait_ge(exp_ready.sem, exp_ready.at(row, i + 1))
            if i < 2:
                pe.wait_ge(p_ev.sem, p_ev.at(row - 1, i + 3))
            else:
                pe.wait_ge(p_ev.sem, p_ev.at(row, i - 1))
            for j in range(i + 1):
                mm = pe.transpose(tbank[:, i % 2, j * P:(j + 1) * P], pr[:, i % 2, j * P:(j + 1) * P], k.ident[:])
            mm.then_inc(p_mm.sem, 1)

        def values(pe, row, i):
            if i == 0:
                pe.wait_ge(qkv_ev.sem, qkv_ev.at(row, QKV))
            pe.wait_ge(p_ev.sem, p_ev.at(row, i + 1))
            if i < 2:
                pe.wait_ge(x3_ready.sem, x3_ready.at(row - 1, i + 3))
            else:
                pe.wait_ge(x3_ready.sem, x3_ready.at(row, i - 1))
            for j in range(i + 1):
                mm = pe.matmul(obank[:, i % 2, 0:C], prT[:, i % 2, j * P:(j + 1) * P], v[:, j, :], start=(j == 0),
                               stop=(j == i))
            mm.then_inc(o_mm.sem, 1)

        def rows(eng, one_row):
            one_row(0, 0)
            one_row(1, 1)
            with eng.Fori(1, B // 2 - 1) as pair:
                one_row(2 * pair, 0)
                one_row(2 * pair + 1, 1)
            one_row(B - 2, 0)
            one_row(B - 1, 1)

        def is_row(row, n):
            return isinstance(row, int) and row == n

        with nc.Block() as block:
            @block.sync
            def _(sp):
                load_x(sp, 0)
                for t, n in ((wq, "w_q"), (wk, "w_k"), (wv, "w_v")):
                    sp.dma_start(t[:], w[n].rearrange("(k p) n -> p k n", p=P)).then_inc(loaded, 16)
                load_x(sp, 1)

                def one_row(row, par):
                    if not (is_row(row, B - 2) or is_row(row, B - 1)):
                        load_x(sp, row + 2)
                    store_x3(sp, row)

                rows(sp, one_row)
                sp.wait_ge(x3_st.sem, x3_st.at(B - 1, 16))

            @block.gpsimd
            def _(pool):
                mix_fetch(pool, mixer, 0, 0, 0)
                norm_rstd(pool, norm, 0)
                mix_fetch(pool, mixer, 1, 1, 0)
                norm_rstd(pool, norm, 1)

                def one_row(row, par):
                    if not (is_row(row, B - 2) or is_row(row, B - 1)):
                        mix_fetch(pool, mixer, row + 2, row + 2, 0)
                    if not is_row(row, 0):
                        for n in range(NT * K):
                            route_send(pool, r, row - 1, n)
                    norm_rstd(pool, r.norm, row)
                    if not (is_row(row, B - 2) or is_row(row, B - 1)):
                        norm_rstd(pool, norm, row + 2)

                rows(pool, one_row)
                for n in range(NT * K):
                    route_send(pool, r, B - 1, n)
                pool.wait_ge(r.sent.sem, r.sent.at(B - 1, 16 * NT * K))

            @block.scalar
            def _(act):
                for c in range(NC):
                    turned(act, 0, c)
                for job in range(2 * NC):
                    qkv_copy(act, 0, job)

                def one_row(row, par):
                    probs(act, row, 0)
                    probs(act, row, 1)
                    qkv_copy(act, row, 2 * NC)
                    if not is_row(row, 0):
                        route_exp(act, r, row - 1)
                    probs_turned(act, row, 0)
                    probs(act, row, 2)
                    qkv_copy(act, row, 2 * NC + 1)
                    probs_turned(act, row, 1)
                    probs_turned(act, row, 2)
                    probs(act, row, 3)
                    probs_turned(act, row, 3)
                    if not is_row(row, B - 1):
                        for c in range(NC):
                            turned(act, row + 1, c)
                        for job in range(2 * NC):
                            qkv_copy(act, row + 1, job)
                    for c in range(NC):
                        route_turned(act, r, row, c)

                rows(act, one_row)
                route_exp(act, r, B - 1)

            @block.vector
            def _(dve):
                add_ffn(dve, 0, 0)
                norm_stats(dve, norm, x2[:, 0], 0)
                norm_apply(dve, norm, x2[:, 0], xn, 0)
                add_ffn(dve, 1, 1)
                norm_stats(dve, norm, x2[:, 1], 1)

                def one_row(row, par):
                    row_max(dve, row, 0)
                    row_max(dve, row, 1)
                    if not is_row(row, 0):
                        route_best(dve, r, row - 1)
                    if not is_row(row, 0):
                        route_slots(dve, r, row - 1)
                    row_max(dve, row, 2)
                    add_attention(dve, row, par, 0)
                    if not is_row(row, B - 1):
                        dve.wait_ge(t_mm.sem, t_mm.at(row, NC))
                        norm_apply(dve, norm, x2[:, 1 - par], xn, row + 1)
                    row_max(dve, row, 3)
                    for i in range(1, NT):
                        add_attention(dve, row, par, i)
                    dve.wait_ge(x3_ready.sem, x3_ready.at(row, NT))
                    norm_stats(dve, r.norm, x3, row)
                    route_norm(dve, r, x3, row)
                    if not (is_row(row, B - 2) or is_row(row, B - 1)):
                        add_ffn(dve, row + 2, par)
                    if not (is_row(row, B - 2) or is_row(row, B - 1)):
                        norm_stats(dve, norm, x2[:, par], row + 2)

                rows(dve, one_row)
                route_best(dve, r, B - 1)
                route_slots(dve, r, B - 1)

            @block.tensor
            def _(pe):
                for c in range(NC):
                    turn(pe, 0, c)
                pe.wait_ge(loaded, 48)
                for job in range(2 * NC):
                    qkv(pe, 0, job)

                def one_row(row, par):
                    scores(pe, row, 0)
                    scores(pe, row, 1)
                    if not is_row(row, 0):
                        route_logits(pe, r, row - 1)
                    qkv(pe, row, 2 * NC)
                    if not is_row(row, 0):
                        route_places(pe, r, row - 1)
                    turn_probs(pe, row, 0)
                    scores(pe, row, 2)
                    qkv(pe, row, 2 * NC + 1)
                    turn_probs(pe, row, 1)
                    values(pe, row, 0)
                    turn_probs(pe, row, 2)
                    scores(pe, row, 3)
                    values(pe, row, 1)
                    values(pe, row, 2)
                    turn_probs(pe, row, 3)
                    if not is_row(row, B - 1):
                        for c in range(NC):
                            turn(pe, row + 1, c)
                    values(pe, row, 3)
                    if not is_row(row, B - 1):
                        for job in range(2 * NC):
                            qkv(pe, row + 1, job)
                    for c in range(NC):
                        if is_row(row, B - 1):
                            pe.wait_ge(r.steps.sem, r.steps.at(row - 1, PLACES))
                        else:
                            pe.wait_ge(qkv_ev.sem, qkv_ev.at(row + 1, 2 * NC - 1 + c))
                        route_transpose(pe, r, row, c)

                rows(pe, one_row)
                route_logits(pe, r, B - 1)
                route_places(pe, r, B - 1)


def combine_phase(nc, k, out):
    with ExitStack() as ctx:
        def sb(name, shape, dt=F32):
            return ctx.enter_context(nc.sbuf_tensor("c_" + name, shape, dt))

        def sem(name):
            return ctx.enter_context(nc.semaphore("c_" + name))

        xa, xo = sb("xa", [P, 2, NT, C]), sb("xo", [P, 2, NT, C])
        mixer = Mixer(sb, sem, "mix", k, 2, 2, first=HALF)
        x_ld = [Count(sem(f"x_ld{i}"), 16) for i in range(2)]
        stored = [Count(sem(f"stored{i}"), 16, ahead=1) for i in range(2)]

        with nc.Block() as block:
            @block.sync
            def _(sp):
                with sp.Fori(0, HALF // 2) as pair:
                    for par in range(2):
                        turn = 2 * pair + par
                        sp.wait_ge(mixer.steps.sem, mixer.steps.at(turn - 2, 1 + NT * K))
                        sp.dma_start(xa[:, par], k.x3[bass.ds(turn + HALF, 1)].rearrange("a (j p) c -> p (a j) c", p=P)) \
                            .then_inc(x_ld[par].sem, 16)

            @block.gpsimd
            def _(pool):
                with pool.Fori(0, HALF // 2) as pair:
                    for par in range(2):
                        mix_fetch(pool, mixer, 2 * pair + par + HALF, pair, par)

            @block.vector
            def _(dve):
                mixer.steps.grant(dve)
                with dve.Fori(0, HALF // 2) as pair:
                    for par in range(2):
                        dve.wait_ge(x_ld[par].sem, x_ld[par].at(pair, 16))
                        dve.wait_ge(stored[par].sem, stored[par].at(pair - 1, 16))
                        mix(dve, mixer, 2 * pair + par + HALF, pair, par, xa[:, par], xo[:, par])

            @block.scalar
            def _(act):
                for par in range(2):
                    stored[par].grant(act)
                with act.Fori(0, HALF // 2) as pair:
                    for par in range(2):
                        turn = 2 * pair + par
                        act.wait_ge(mixer.steps.sem, mixer.steps.at(turn, 1 + NT * K))
                        act.dma_start(out[bass.ds(turn + HALF, 1)].rearrange("a (j p) c -> p (a j) c", p=P), xo[:, par]) \
                            .then_inc(stored[par].sem, 16)
                for par in range(2):
                    act.wait_ge(stored[par].sem, stored[par].at(HALF // 2 - 1, 16))


SHORT = {"L0_attn_a_": "", "L0_attn_b_": "", "L0_ffn_": ""}


def short(name):
    for head in SHORT:
        if name.startswith(head):
            return name[len(head):]
    return name


def build(nc, arrays):
    w = {}
    for name, a in arrays.items():
        w[short(name)] = nc.dram_tensor(name, a.shape, mybir.dt.from_np(a.dtype), kind="ExternalInput").ap()
    out = nc.dram_tensor("out", (B, T, C), F32, kind="ExternalOutput").ap()
    with ExitStack() as ctx:
        ctx.enter_context(nc.allow_non_contiguous_dma(reason="short bias vectors, once"))
        k = build_kit(nc, ctx, w)
        mamba_phase(nc, k, w)
        experts_phase(nc, k, w, "ffn1")
        attention_phase(nc, k, w)
        experts_phase(nc, k, w, "ffn2", out)
        combine_phase(nc, k, out)


def kernel(**inputs):
    import concourse.bacc as bacc
    from concourse.bass_utils import run_bass_kernel_spmd

    nc = bacc.Bacc("TRN2", target_bir_lowering=False, num_devices=1)
    arrays = {name: np.ascontiguousarray(a) for name, a in inputs.items()}
    build(nc, arrays)
    r = run_bass_kernel_spmd(nc, [arrays], core_ids=[0])
    return r.results[0]["out"]
```

```python
from contextlib import ExitStack

import numpy as np
import concourse.bass as bass
from concourse import mybir

ACT = mybir.ActivationFunctionType
ALU = mybir.AluOpType
AX = mybir.AxisListType
F32 = mybir.dt.float32
BF16 = mybir.dt.bfloat16
F32R = mybir.dt.float32r
U32 = mybir.dt.uint32

P = 128
B, T, C = 16, 512, 256
NT, NC = T // P, C // P
DI, NS, DC = 512, 16, 4
ND = DI // P
E, H, K = 8, 1024, 2
NH = H // P
CAP = int(T / E * 1.25)
HALF = B // 2
ROWS = HALF * CAP
NR = ROWS // P
SLOTS = 2 * E * ROWS
EPS = 1e-5
FAR = float(2 * SLOTS)
RESET = 1.0e4

GN = 4
NG = NS // GN
SN = 2
STEPS = NS // SN * ND
DEEP = 4
ADDED = (5, 9, 17, 18, 19, 20, 21, 22, 23, 26, 27)
XW = DI + 48


class Count:

    def __init__(self, sem, per, ahead=0):
        self.sem, self.per, self.ahead = sem, per, ahead

    def grant(self, eng):
        eng.sem_inc(self.sem, self.per * self.ahead)

    def at(self, row, n):
        value = (row + self.ahead) * self.per + n
        return max(value, 0) if isinstance(value, int) else value


LOGITS = 1
MASK = LOGITS + 2 * NT + 2
PLACES = MASK + 3
ROUTE_STEPS = PLACES + 9


class Router:

    def __init__(self, sb, sem, k, xbanks, lbank, pbank, copies=1):
        self.copies = copies
        self.k, self.xbanks, self.lbank, self.pbank = k, xbanks, lbank, pbank
        self.norm = Norm(sb, sem, k, "r_norm")
        self.xn, self.xnT = sb("r_xn", [P, copies, NT, C]), sb("r_xnT", [P, NC, T])
        self.logits, self.best = sb("r_logits", [P, NT, E]), sb("r_best", [P, NT, 8])
        self.which, self.whichf = sb("r_which", [P, NT, 8], U32), sb("r_whichf", [P, NT, K])
        self.mask, self.maskb = sb("r_mask", [P, NT, K, E]), sb("r_maskb", [P, NT, E], BF16)
        self.below, self.e8 = sb("r_below", [P, NT, 8]), sb("r_e8", [P, NT, 8])
        self.esum, self.einv = sb("r_esum", [P, NT]), sb("r_einv", [P, NT])
        self.prob = sb("r_prob", [P, NT, K])
        self.mpos, self.pos = sb("r_mpos", [P, NT, K, E]), sb("r_pos", [P, NT, K])
        self.keep, self.cpos = sb("r_keep", [P, NT, K]), sb("r_cpos", [P, NT, K])
        self.slot, self.dead = sb("r_slot", [P, NT, K]), sb("r_dead", [P, NT, K])
        self.send = sb("r_send", [P, NT * K], U32)
        self.steps = Count(sem("r_steps"), ROUTE_STEPS)
        self.held = Count(sem("r_held"), 1)
        self.x_mm, self.x_ev = Count(sem("r_x_mm"), NC), Count(sem("r_x_ev"), NC)
        self.l_mm, self.p_mm = Count(sem("r_l_mm"), 1), Count(sem("r_p_mm"), 1)
        self.mask_ready = Count(sem("r_mask_ready"), 1)
        self.below_ready, self.e8_ready = Count(sem("r_below_ready"), 1), Count(sem("r_e8_ready"), 1)
        self.done = Count(sem("r_done"), 1)
        self.pool_held = Count(sem("r_pool_held"), 1)
        self.sent = Count(sem("r_sent"), 16 * NT * K)


class Norm:

    def __init__(self, sb, sem, k, name):
        self.k = k
        self.stats, self.ln = sb(name + "_stats", [P, NT, 6]), sb(name + "_ln", [P, 6, NT])
        self.steps = Count(sem(name + "_steps"), NT + 6)
        self.rstd_ready = Count(sem(name + "_rstd_ready"), 1)
        self.ready = Count(sem(name + "_ready"), NT)


def norm_stats(dve, n, x, row):
    done = n.steps
    for j in range(NT):
        dve.bn_stats(n.stats[:, j, :], x[:, j, :]).then_inc(done.sem, 1)
    me, m2e, mo, m2o = (n.stats[:, :, i] for i in (1, 2, 4, 5))
    total, diff, sq, mean, var = (n.ln[:, i, :] for i in range(5))
    dve.wait_ge(done.sem, done.at(row, NT))
    dve.tensor_tensor(total, me, mo, ALU.add).then_inc(done.sem, 1)
    dve.tensor_tensor(diff, me, mo, ALU.subtract).then_inc(done.sem, 1)
    dve.scalar_tensor_tensor(sq, m2e, C * EPS, m2o, ALU.add, ALU.add).then_inc(done.sem, 1)
    dve.wait_ge(done.sem, done.at(row, NT + 3))
    dve.tensor_scalar(mean, total, 0.5, None, ALU.mult).then_inc(done.sem, 1)
    dve.scalar_tensor_tensor(diff, diff, 0.25, diff, ALU.mult, ALU.mult).then_inc(done.sem, 1)
    dve.wait_ge(done.sem, done.at(row, NT + 5))
    dve.scalar_tensor_tensor(var, sq, 1.0 / C, diff, ALU.mult, ALU.add).then_inc(done.sem, 1)


def norm_rstd(pool, n, row):
    pool.wait_ge(n.steps.sem, n.steps.at(row, NT + 6))
    pool.tensor_tensor(n.ln[:, 5, :], n.ln[:, 4, :], n.k.minus_half[:], ALU.pow).then_inc(n.rstd_ready.sem, 1)


def norm_apply(dve, n, x, xn, row):
    dve.wait_ge(n.rstd_ready.sem, n.rstd_ready.at(row, 1))
    for j in range(NT):
        dve.tensor_scalar(xn[:, j, :], x[:, j, :], n.ln[:, 3, j:j + 1], n.ln[:, 5, j:j + 1],
                          ALU.subtract, ALU.mult).then_inc(n.ready.sem, 1)


def route_norm(dve, r, x, row, copy=0):
    dve.wait_ge(r.sent.sem, r.sent.at(row - r.copies, 16 * NT * K))
    norm_apply(dve, r.norm, x, r.xn[:, copy], row)


def route_transpose(pe, r, row, k, copy=0):
    pe.wait_ge(r.norm.ready.sem, r.norm.ready.at(row, NT))
    for j in range(NT):
        mm = pe.transpose(r.xbanks[k][:, j * P:(j + 1) * P], r.xn[:, copy, j, k * P:(k + 1) * P], r.k.ident[:])
    mm.then_inc(r.x_mm.sem, 1)


def route_turned(act, r, row, k):
    act.wait_ge(r.x_mm.sem, r.x_mm.at(row, k + 1))
    act.wait_ge(r.l_mm.sem, r.l_mm.at(row - 1, 1))
    act.activation(r.xnT[:, k, :], r.xbanks[k], ACT.Copy).then_inc(r.x_ev.sem, 1)


def route_logits(pe, r, row):
    pe.wait_ge(r.x_ev.sem, r.x_ev.at(row, NC))
    pe.wait_ge(r.done.sem, r.done.at(row - 1, 1))
    for j in range(NT):
        for k in range(NC):
            mm = pe.matmul(r.lbank[:, j * E:(j + 1) * E], r.xnT[:, k, j * P:(j + 1) * P], r.k.w_router[:, k, :],
                           start=(k == 0), stop=(k == NC - 1))
    mm.then_inc(r.l_mm.sem, 1)


def route_best(dve, r, row):
    done = r.steps
    dve.wait_ge(r.l_mm.sem, r.l_mm.at(row, 1))
    dve.tensor_copy(r.logits[:], r.lbank[:, 0:NT * E].rearrange("p (j e) -> p j e", e=E)).then_inc(done.sem, 1)
    dve.wait_ge(done.sem, done.at(row, LOGITS))
    dve.sem_inc(r.held.sem, 1)
    for j in range(NT):
        dve.max(r.best[:, j, :], r.logits[:, j, :]).then_inc(done.sem, 1)
    dve.wait_ge(done.sem, done.at(row, LOGITS + NT))
    dve.sem_inc(r.held.sem, 1)
    for j in range(NT):
        dve.max_index(r.which[:, j, :], r.best[:, j, :], r.logits[:, j, :]).then_inc(done.sem, 1)
    dve.wait_ge(r.e8_ready.sem, r.e8_ready.at(row - 1, 1))
    dve.tensor_tensor(r.below[:], r.best[:], r.best[:, :, 0:1].to_broadcast([P, NT, 8]),
                      ALU.subtract).then_inc(r.below_ready.sem, 1)
    dve.wait_ge(done.sem, done.at(row, LOGITS + 2 * NT))
    dve.tensor_copy(r.whichf[:], r.which[:, :, 0:K]).then_inc(done.sem, 1)
    dve.wait_ge(done.sem, done.at(row, LOGITS + 2 * NT + 1))
    dve.tensor_tensor(r.mask[:], r.k.iota_e[:].unsqueeze(1).unsqueeze(1).to_broadcast([P, NT, K, E]),
                      r.whichf[:].unsqueeze(3).to_broadcast([P, NT, K, E]), ALU.is_equal).then_inc(done.sem, 1)
    dve.wait_ge(done.sem, done.at(row, MASK))
    dve.tensor_tensor(r.maskb[:], r.mask[:, :, 0, :], r.mask[:, :, 1, :], ALU.add).then_inc(r.mask_ready.sem, 1)


def route_exp(act, r, row):
    act.wait_ge(r.below_ready.sem, r.below_ready.at(row, 1))
    act.wait_ge(r.done.sem, r.done.at(row - 1, 1))
    act.activation(r.e8[:], r.below[:], ACT.Exp).then_inc(r.e8_ready.sem, 1)


def route_places(pe, r, row):
    pe.wait_ge(r.mask_ready.sem, r.mask_ready.at(row, 1))
    for j in range(NT):
        for i in range(j + 1):
            mm = pe.matmul(r.pbank[:, j * E:(j + 1) * E], r.k.ones[:] if i < j else r.k.earlier[:], r.maskb[:, i, :],
                           start=(i == 0), stop=(i == j))
    mm.then_inc(r.p_mm.sem, 1)


def route_slots(dve, r, row):
    done = r.steps
    dve.wait_ge(r.e8_ready.sem, r.e8_ready.at(row, 1))
    dve.tensor_reduce(r.esum[:], r.e8[:], AX.X, ALU.add).then_inc(done.sem, 1)
    dve.wait_ge(done.sem, done.at(row, MASK + 1))
    dve.reciprocal(r.einv[:], r.esum[:]).then_inc(done.sem, 1)
    dve.wait_ge(r.p_mm.sem, r.p_mm.at(row, 1))
    places = r.pbank[:, 0:NT * E].rearrange("p (j e) -> p j e", e=E).unsqueeze(2).to_broadcast([P, NT, K, E])
    dve.tensor_tensor(r.mpos[:], r.mask[:], places, ALU.mult).then_inc(done.sem, 1)
    dve.wait_ge(done.sem, done.at(row, MASK + 2))
    dve.tensor_tensor(r.prob[:], r.e8[:, :, 0:K], r.einv[:].unsqueeze(2).to_broadcast([P, NT, K]),
                      ALU.mult).then_inc(done.sem, 1)
    dve.wait_ge(done.sem, done.at(row, PLACES))
    dve.tensor_reduce(r.pos[:], r.mpos[:], AX.X, ALU.add).then_inc(done.sem, 1)
    dve.wait_ge(done.sem, done.at(row, PLACES + 2))
    dve.tensor_scalar(r.keep[:], r.pos[:], float(CAP), None, ALU.is_lt).then_inc(done.sem, 1)
    dve.tensor_scalar(r.cpos[:], r.pos[:], float(CAP - 1), None, ALU.min).then_inc(done.sem, 1)
    dve.tensor_scalar(r.dead[:], r.pos[:], float(CAP), FAR, ALU.is_ge, ALU.mult).then_inc(done.sem, 1)
    dve.wait_ge(done.sem, done.at(row, PLACES + 5))
    dve.scalar_tensor_tensor(r.slot[:], r.whichf[:], float(ROWS), r.cpos[:], ALU.mult, ALU.add).then_inc(done.sem, 1)
    base = r.k.row_base[:, bass.ds(row, 1)].unsqueeze(2).to_broadcast([P, NT, K])
    dve.wait_ge(done.sem, done.at(row, PLACES + 6))
    dve.tensor_tensor(r.slot[:], r.slot[:], base, ALU.add).then_inc(done.sem, 1)
    share = r.k.share[:, bass.ds(row, 1), :].rearrange("p a (j k) -> p (a j) k", k=K)
    fetch = r.k.fetch[:, bass.ds(row, 1), :].rearrange("p a (j k) -> p (a j) k", k=K)
    dve.tensor_tensor(share, r.prob[:], r.keep[:], ALU.mult).then_inc(done.sem, 1)
    dve.wait_ge(done.sem, done.at(row, PLACES + 7))
    dve.tensor_copy(fetch, r.slot[:]).then_inc(done.sem, 1)
    dve.wait_ge(r.sent.sem, r.sent.at(row - 1, 16 * NT * K))
    dve.tensor_tensor(r.send[:].rearrange("p (j k) -> p j k", k=K), r.slot[:], r.dead[:],
                      ALU.add).then_inc(r.done.sem, 1)


def route_send(pool, r, row, n, copy=0):
    if n == 0:
        pool.wait_ge(r.done.sem, r.done.at(row, 1))
        pool.sem_inc(r.pool_held.sem, 1)
    pool.indirect_dma_start(
        r.k.slots, bass.IndirectOffsetOnAxis(ap=r.send[:, n:n + 1], axis=0), r.xn[:, copy, n // K, :], None,
        bounds_check=SLOTS - 1, oob_is_err=False).then_inc(r.sent.sem, 16)


class Kit:
    pass


def columns(ap):
    return ap.rearrange("(m p) -> p m", p=P)


def build_kit(nc, ctx, w):
    k = Kit()

    def sb(name, shape, dt=F32):
        return ctx.enter_context(nc.sbuf_tensor(name, shape, dt))

    def sem(name):
        return ctx.enter_context(nc.semaphore(name))

    k.ident, k.identb = sb("ident", [P, P]), sb("identb", [P, P], BF16)
    k.earlier, k.ones = sb("earlier", [P, P], BF16), sb("ones", [P, P], BF16)
    k.future = sb("future", [P, T], BF16)
    k.iota_e, k.row_base = sb("iota_e", [P, E]), sb("row_base", [P, B])
    k.minus_half = sb("minus_half", [P, NT])
    k.w_router = sb("w_router", [P, NC, E])
    k.b1 = sb("b1", [P, 2 * E, NH])
    k.share, k.fetch = sb("share", [P, B, NT * K]), sb("fetch", [P, B, NT * K], U32)
    k.zero = sb("zero", [P, 4 * C])

    def dram(name, shape):
        return nc.dram_tensor(name, shape, F32, kind="Internal").ap()

    k.slots, k.results = dram("slots", (SLOTS, C)), dram("results", (SLOTS, C))
    k.x1, k.x3 = dram("x_after_mamba", (B, T, C)), dram("x_after_attention", (B, T, C))
    k.b_rows = dram("b_rows", (2, NS, T))
    made, shaped = sem("made"), sem("shaped")

    with nc.Block() as block:
        @block.gpsimd
        def _(pool):
            for t, v in ((k.ident, 0.0), (k.identb, 0.0), (k.earlier, 0.0), (k.ones, 1.0), (k.future, 0.0),
                         (k.minus_half, -0.5), (k.zero, 0.0)):
                pool.memset(t[:], v).then_inc(made, 1)
            pool.wait_ge(made, 7)
            for t in (k.ident, k.identb):
                pool.affine_select(out=t[:], in_=t[:], compare_op=ALU.not_equal, fill=1.0, base=0,
                                   pattern=[[-1, P]], channel_multiplier=1).then_inc(shaped, 1)
            pool.affine_select(out=k.earlier[:], in_=k.earlier[:], compare_op=ALU.is_ge, fill=1.0, base=0,
                               pattern=[[-1, P]], channel_multiplier=1).then_inc(shaped, 1)
            pool.affine_select(out=k.future[:, T - P:], in_=k.future[:, T - P:], compare_op=ALU.is_ge, fill=-1.0e30, base=0,
                               pattern=[[-1, P]], channel_multiplier=1).then_inc(shaped, 1)
            pool.iota(k.iota_e[:], [[1, E]], base=0, channel_multiplier=0,
                      allow_small_or_imprecise_dtypes=True).then_inc(shaped, 1)
            pool.iota(k.row_base[:], [[E * ROWS, 2], [CAP, HALF]], base=0, channel_multiplier=0,
                      allow_small_or_imprecise_dtypes=True).then_inc(shaped, 1)
            pool.wait_ge(shaped, 6)
    return k


def mamba_phase(nc, k, w):
    with ExitStack() as ctx:
        def sb(name, shape, dt=F32):
            return ctx.enter_context(nc.sbuf_tensor(name, shape, dt))

        def sem(name):
            return ctx.enter_context(nc.semaphore(name))

        w_in, w_x = sb("w_in", [P, NC, 2 * DI]), sb("w_x", [P, ND, XW])
        w_dt, w_out = sb("w_dt", [32, DI]), sb("w_out", [P, ND, C])
        b_in, b_z, b_u = sb("b_in", [P, 2 * ND]), sb("b_z", [P, ND]), sb("b_u", [P, ND])
        b_db, w_conv, b_conv = sb("b_db", [48, 1]), sb("w_conv", [P, ND, DC]), sb("b_conv", [P, ND])
        d_skip, b_out = sb("d_skip", [P, ND]), sb("b_out", [P, C])
        xt, xnT = sb("xt", [P, NT, C]), sb("xnT", [P, NC, T])
        norm = Norm(sb, sem, k, "norm")
        xc = sb("xc", [P, ND, DC - 1 + T])
        hx, th = sb("hx", [P, ND, T]), sb("th", [P, 2, T])
        db = sb("db", [48, T])
        delta, du, u = (sb(n, [P, 2, ND, T]) for n in ("delta", "du", "u"))
        sz = sb("sz", [P, 2, ND, T])
        bb = sb("bb", [P, 2, GN, T])
        da, dbu, hs = (sb(n, [P, DEEP, SN, T]) for n in ("da", "dbu", "hs"))
        x1 = sb("x1", [P, NT, C])
        ys = ctx.enter_context(nc.psum_tensor("ys", [P, ND, T], F32))
        ring = ctx.enter_context(nc.psum_tensor("ring", [P, 2, T], F32))
        ob = ctx.enter_context(nc.psum_tensor("ob", [P, 2, T], F32))
        tail_of_xc = xc[:, :, DC - 1:]

        r = Router(sb, sem, k, [ob[:, 0, :], ob[:, 1, :]], ob[:, 0, :], ob[:, 1, :])

        first_loaded, loaded, route_loaded = sem("first_loaded"), sem("loaded"), sem("route_loaded")
        cleared, dt_cleared, halved = sem("cleared"), sem("dt_cleared"), sem("halved")
        bias_one, zeroed = sem("bias_one"), sem("zeroed")
        x_ld, x1_ld, x1_st = Count(sem("x_ld"), 16), Count(sem("x1_ld"), 16), Count(sem("x1_st"), 16)
        b_st, sp_held = Count(sem("b_st"), 16), sem("sp_held")
        bb_ld = [Count(sem(f"bb_ld{g}"), 16) for g in range(NG)]
        x1_based = Count(sem("x1_based"), 1)
        TJ, IJ, SJ = 0, NC, NC + ND
        DJ = SJ + 2
        UJ = [SJ + 1] + [DJ + ND + m for m in range(ND - 1)]
        ZJ = UJ[-1] + 1
        JOBS = ZJ + ND
        job_mm, job_ev = Count(sem("job_mm"), JOBS), Count(sem("job_ev"), JOBS)
        thx_ready, xc_ready = Count(sem("thx_ready"), ND), Count(sem("xc_ready"), ND)
        thz_ready, sz_ready = Count(sem("thz_ready"), ND), Count(sem("sz_ready"), ND)
        conv_tap, conv = Count(sem("conv_tap"), ND), Count(sem("conv"), ND * (DC - 1))
        exp_done, log_done = Count(sem("exp_done"), 1), Count(sem("log_done"), 1)
        delta_ready, du_ready = Count(sem("delta_ready"), ND), Count(sem("du_ready"), ND)
        reset_ready = Count(sem("reset_ready"), ND)
        da_ready, dbu_ready = Count(sem("da_ready"), STEPS), Count(sem("dbu_ready"), STEPS)
        scanned, summed = Count(sem("scanned"), STEPS), Count(sem("summed"), STEPS)
        added = Count(sem("added"), len(ADDED))
        ys_read, y2_ready = Count(sem("ys_read"), ND), Count(sem("y2_ready"), ND)
        o_mm, x1_ready = Count(sem("o_mm"), 2), Count(sem("x1_ready"), 2)

        def load_first_consts(sp):
            for dst, src in ((w_in[:], w["in_proj_w"].rearrange("(k p) n -> p k n", p=P)),
                             (b_in[:], columns(w["in_proj_b"])),
                             (w_conv[:], w["conv_w"].rearrange("(m p) a k -> p m (a k)", p=P)),
                             (b_conv[:], columns(w["conv_b"]))):
                sp.dma_start(dst, src).then_inc(first_loaded, 16)

        FIRST_CONSTS, CONSTS, ROUTE_CONSTS = 4, 11, 1 + 2 * E

        def load_consts(sp):
            for dst, src in ((w_x[:, :, 0:DI], w["x_proj_w"][:, 2 * NS:].rearrange("(k p) n -> p k n", p=P)),
                             (w_x[:, :, DI:DI + NS], w["x_proj_w"][:, 0:NS].rearrange("(k p) n -> p k n", p=P)),
                             (w_x[:, :, DI + 32:], w["x_proj_w"][:, NS:2 * NS].rearrange("(k p) n -> p k n", p=P)),
                             (b_u[:], columns(w["x_proj_b"][2 * NS:])), (d_skip[:], columns(w["D"])),
                             (b_out[:], w["out_proj_b"].partition_broadcast(P)),
                             (w_out[:], w["out_proj_w"].rearrange("(k p) n -> p k n", p=P))):
                sp.dma_start(dst, src).then_inc(loaded, 16)
            sp.wait_ge(dt_cleared, 1)
            sp.dma_start(w_dt[0:NS, :], w["dt_proj_w"]).then_inc(loaded, 16)
            sp.dma_start(w_dt[NS:NS + 1, :], w["dt_proj_b"].rearrange("(a n) -> a n", a=1)).then_inc(loaded, 16)
            sp.wait_ge(bias_one, 2)
            sp.dma_start(b_db[0:NS, :], w["x_proj_b"][0:NS].rearrange("(n a) -> n a", a=1)).then_inc(loaded, 16)
            sp.dma_start(b_db[32:48, :], w["x_proj_b"][NS:2 * NS].rearrange("(n a) -> n a", a=1)).then_inc(loaded, 16)

        def load_route_consts(sp):
            sp.dma_start(k.w_router[:], w["Wr"].rearrange("(k p) e -> p k e", p=P)).then_inc(route_loaded, 16)
            for turn in range(2 * E):
                sp.dma_start(k.b1[:, turn, :], columns(w["b1"][turn % E])).then_inc(route_loaded, 16)

        def load_x(sp, row):
            sp.wait_ge(job_mm.sem, job_mm.at(row - 1, TJ + NC))
            sp.dma_start(xt[:], w["x"][row].rearrange("(j p) c -> p j c", p=P)).then_inc(x_ld.sem, 16)

        def load_x1(sp, row):
            sp.wait_ge(r.norm.ready.sem, r.norm.ready.at(row - 1, NT))
            sp.wait_ge(x1_st.sem, x1_st.at(row - 1, 16))
            sp.dma_start(x1[:], w["x"][row].rearrange("(j p) c -> p j c", p=P)).then_inc(x1_ld.sem, 16)

        def store_x1(sp, row):
            sp.wait_ge(x1_ready.sem, x1_ready.at(row, 2))
            sp.dma_start(k.x1[row].rearrange("(j p) c -> p j c", p=P), x1[:]).then_inc(x1_st.sem, 16)

        ZR = 4 * P
        ZN = SLOTS // ZR

        def clear_slots(sp, half):
            for i in range(half * ZN // 2, (half + 1) * ZN // 2):
                sp.dma_start(k.slots[i * ZR:(i + 1) * ZR].rearrange("(p r) c -> p (r c)", p=P),
                             k.zero[:]).then_inc(zeroed, 16)

        def store_b(sp, row, par):
            sp.wait_ge(job_ev.sem, job_ev.at(row, SJ + 1))
            sp.dma_start(k.b_rows[par], db[32:48, :]).then_inc(b_st.sem, 16)

        def spread_b(sp, row, par, g):
            if g == 0:
                sp.wait_ge(b_st.sem, b_st.at(row, 16))
                sp.sem_inc(sp_held, 1)
            sp.wait_ge(dbu_ready.sem, dbu_ready.at(row, (g - 1) * STEPS // NG))
            src = k.b_rows[par, g * GN:(g + 1) * GN, :].rearrange("n t -> (n t)").partition_broadcast(P)
            sp.dma_start(bb[:, g % 2].rearrange("p n t -> p (n t)"), src).then_inc(bb_ld[g].sem, 16)

        def add_out_bias(pool, row):
            pool.wait_ge(x1_ld.sem, x1_ld.at(row, 16))
            pool.tensor_tensor(x1[:], x1[:], b_out[:].unsqueeze(1).to_broadcast([P, NT, C]),
                               ALU.add).then_inc(x1_based.sem, 1)

        def step_of(s):
            return s // (STEPS // NG), s % (STEPS // NG) // (GN // SN), s % (GN // SN)

        def input_step(pool, row, par, s):
            g, dt, part = step_of(s)
            if g == 0 and part == 0:
                pool.wait_ge(du_ready.sem, du_ready.at(row, dt + 1))
            if dt == 0 and part == 0:
                pool.wait_ge(bb_ld[g].sem, bb_ld[g].at(row, 16))
            pool.wait_ge(scanned.sem, scanned.at(row, s + 1 - DEEP))
            pool.tensor_tensor(dbu[:, s % DEEP], du[:, par, dt, :].unsqueeze(1).to_broadcast([P, SN, T]),
                               bb[:, g % 2, part * SN:(part + 1) * SN, :], ALU.mult).then_inc(dbu_ready.sem, 1)

        def turned(act, row, par, c):
            act.wait_ge(job_mm.sem, job_mm.at(row, TJ + c + 1))
            act.activation(xnT[:, c, :], ring[:, (par + TJ + c) % 2, :], ACT.Copy).then_inc(job_ev.sem, 1)

        def conv_input(act, row, par, m):
            act.wait_ge(job_mm.sem, job_mm.at(row, IJ + m + 1))
            act.wait_ge(delta_ready.sem, delta_ready.at(row - 1, ND))
            act.activation(xc[:, m, DC - 1:], ring[:, (par + IJ + m) % 2, :], ACT.Identity,
                           bias=b_in[:, m:m + 1]).then_inc(job_ev.sem, 1)

        def conv_first(act, row, m):
            act.wait_ge(job_ev.sem, job_ev.at(row, IJ + m + 1))
            act.wait_ge(job_mm.sem, job_mm.at(row - 1, UJ[-1] + 1))
            act.activation(hx[:, m, :], xc[:, m, 0:T], ACT.Identity, bias=b_conv[:, m:m + 1],
                           scale=w_conv[:, m, 0:1]).then_inc(conv_tap.sem, 1)

        def tanh_x(act, row, m):
            act.wait_ge(conv.sem, conv.at(row, (DC - 1) * (m + 1)))
            if m < 2:
                act.wait_ge(sz_ready.sem, sz_ready.at(row - 1, m + 3))
            else:
                act.wait_ge(xc_ready.sem, xc_ready.at(row, m - 1))
            act.activation(th[:, m % 2, :], hx[:, m, :], ACT.Tanh).then_inc(thx_ready.sem, 1)

        def gate_input(act, row, par, m):
            act.wait_ge(job_mm.sem, job_mm.at(row, ZJ + m + 1))
            act.wait_ge(o_mm.sem, o_mm.at(row - 2, 2))
            act.activation(sz[:, par, m, :], ring[:, (par + ZJ + m) % 2, :], ACT.Identity, bias=b_z[:, m:m + 1],
                           scale=0.5).then_inc(job_ev.sem, 1)

        def tanh_z(act, row, par, m):
            act.wait_ge(job_ev.sem, job_ev.at(row, ZJ + m + 1))
            if m < 2:
                act.wait_ge(xc_ready.sem, xc_ready.at(row, m + 3))
            else:
                act.wait_ge(sz_ready.sem, sz_ready.at(row, m - 1))
            act.activation(th[:, m % 2, :], sz[:, par, m, :], ACT.Tanh).then_inc(thz_ready.sem, 1)

        def delta_b(act, row, par):
            act.wait_ge(job_mm.sem, job_mm.at(row, SJ + 1))
            act.wait_ge(b_st.sem, b_st.at(row - 1, 16))
            act.activation(db[:], ring[0:48, (par + SJ) % 2, :], ACT.Identity, bias=b_db[:]).then_inc(job_ev.sem, 1)

        def u_bias(act, row, par, m):
            act.wait_ge(job_mm.sem, job_mm.at(row, UJ[m] + 1))
            act.wait_ge(ys_read.sem, ys_read.at(row - 2, ND))
            act.activation(u[:, par, m, :], ring[:, (par + UJ[m]) % 2, :], ACT.Identity,
                           bias=b_u[:, m:m + 1]).then_inc(job_ev.sem, 1)

        def step_size(act, row, par, m):
            act.wait_ge(job_mm.sem, job_mm.at(row, DJ + m + 1))
            act.activation(tail_of_xc[:, m, :], ring[:, (par + DJ + m) % 2, :], ACT.Abs)
            act.activation(delta[:, par, m, :], ring[:, (par + DJ + m) % 2, :], ACT.Relu).then_inc(job_ev.sem, 1)

        def exp_part(act, row):
            act.wait_ge(job_ev.sem, job_ev.at(row, DJ + ND))
            act.activation(tail_of_xc, tail_of_xc, ACT.Exp, scale=-1.0).then_inc(exp_done.sem, 1)

        def log_part(act, row):
            act.wait_ge(exp_done.sem, exp_done.at(row, 1))
            act.activation(tail_of_xc, tail_of_xc, ACT.Ln, bias=1.0).then_inc(log_done.sem, 1)

        def decay_step(act, row, par, s):
            g, dt, part = step_of(s)
            if g == 0 and part == 0:
                act.wait_ge(reset_ready.sem, reset_ready.at(row, dt + 1))
            act.wait_ge(scanned.sem, scanned.at(row, s + 1 - DEEP))
            for i in range(SN):
                ins = act.activation(da[:, s % DEEP, i, :], delta[:, par, dt, :], ACT.Exp,
                                     scale=-float(g * GN + part * SN + i + 1))
            ins.then_inc(da_ready.sem, 1)

        def conv_step(dve, row, m):
            dve.wait_ge(conv_tap.sem, conv_tap.at(row, m + 1))
            for t in range(1, DC):
                if t > 1:
                    dve.wait_ge(conv.sem, conv.at(row, (DC - 1) * m + t - 1))
                dve.scalar_tensor_tensor(hx[:, m, :], xc[:, m, t:t + T], w_conv[:, m, t:t + 1], hx[:, m, :],
                                         ALU.mult, ALU.add).then_inc(conv.sem, 1)

        def silu_x(dve, row, m):
            dve.wait_ge(thx_ready.sem, thx_ready.at(row, m + 1))
            dve.scalar_tensor_tensor(hx[:, m, :], th[:, m % 2, :], 1.0, hx[:, m, :], ALU.add,
                                     ALU.mult).then_inc(xc_ready.sem, 1)

        def silu_z(dve, row, par, m):
            dve.wait_ge(thz_ready.sem, thz_ready.at(row, m + 1))
            dve.scalar_tensor_tensor(sz[:, par, m, :], th[:, m % 2, :], 1.0, sz[:, par, m, :], ALU.add,
                                     ALU.mult).then_inc(sz_ready.sem, 1)

        def softplus(dve, row, par, m):
            dve.wait_ge(log_done.sem, log_done.at(row, 1))
            dve.tensor_tensor(delta[:, par, m, :], delta[:, par, m, :], tail_of_xc[:, m, :],
                              ALU.add).then_inc(delta_ready.sem, 1)

        def step_input(dve, row, par, m):
            dve.wait_ge(delta_ready.sem, delta_ready.at(row, m + 1))
            dve.wait_ge(job_ev.sem, job_ev.at(row, UJ[m] + 1))
            dve.wait_ge(dbu_ready.sem, dbu_ready.at(row - 2, STEPS))
            dve.tensor_tensor(du[:, par, m, :], delta[:, par, m, :], u[:, par, m, :], ALU.mult).then_inc(du_ready.sem, 1)
            dve.wait_ge(du_ready.sem, du_ready.at(row, m + 1))
            dve.memset(delta[:, par, m, 0:1], RESET).then_inc(reset_ready.sem, 1)

        def scan_step(dve, row, s):
            dve.wait_ge(da_ready.sem, da_ready.at(row, s + 1))
            dve.wait_ge(dbu_ready.sem, dbu_ready.at(row, s + 1))
            dve.wait_ge(summed.sem, summed.at(row, s + 1 - DEEP))
            flat = [t[:, s % DEEP].rearrange("p n t -> p (n t)") for t in (hs, da, dbu)]
            dve.tensor_tensor_scan(flat[0], flat[1], flat[2], 0.0, ALU.mult, ALU.add).then_inc(scanned.sem, 1)

        def add_states(dve, row, s):
            dve.wait_ge(scanned.sem, scanned.at(row, s + 1))
            dve.tensor_tensor(hs[:, s % DEEP, 0, :], hs[:, s % DEEP, 0, :], hs[:, s % DEEP, 1, :],
                              ALU.add).then_inc(added.sem, 1)

        def gate(dve, row, par, dt):
            dve.wait_ge(summed.sem, summed.at(row, STEPS - STEPS // NG + (GN // SN) * (dt + 1)))
            dve.scalar_tensor_tensor(u[:, par, dt, :], u[:, par, dt, :], d_skip[:, dt:dt + 1], ys[:, dt, :], ALU.mult,
                                     ALU.add).then_inc(ys_read.sem, 1)
            dve.wait_ge(ys_read.sem, ys_read.at(row, dt + 1))
            dve.wait_ge(sz_ready.sem, sz_ready.at(row, dt + 1))
            dve.tensor_tensor(sz[:, par, dt, :], u[:, par, dt, :], sz[:, par, dt, :], ALU.mult).then_inc(y2_ready.sem, 1)

        def residual(dve, row, h):
            dve.wait_ge(o_mm.sem, o_mm.at(row, h + 1))
            dve.wait_ge(x1_based.sem, x1_based.at(row, 1))
            dve.tensor_tensor(x1[:, 2 * h:2 * h + 2, :], ob[:, h, :].rearrange("p (j c) -> p j c", c=C),
                              x1[:, 2 * h:2 * h + 2, :], ALU.add).then_inc(x1_ready.sem, 1)

        def route_stats(dve, row):
            dve.wait_ge(x1_ready.sem, x1_ready.at(row, 2))
            norm_stats(dve, r.norm, x1, row)

        def job_bank(pe, row, par, job):
            pe.wait_ge(job_ev.sem, job_ev.at(row, job - 1))
            return ring[:, (par + job) % 2, :]

        def turn(pe, row, par, c):
            bank = job_bank(pe, row, par, TJ + c)
            pe.wait_ge(norm.ready.sem, norm.ready.at(row, NT))
            for j in range(NT):
                mm = pe.transpose(bank[:, j * P:(j + 1) * P], xt[:, j, c * P:(c + 1) * P], k.ident[:])
            mm.then_inc(job_mm.sem, 1)

        def in_proj(pe, row, par, job, m):
            bank = job_bank(pe, row, par, job)
            pe.wait_ge(job_ev.sem, job_ev.at(row, TJ + NC))
            for c in range(NC):
                mm = pe.matmul(bank, w_in[:, c, m * P:(m + 1) * P], xnT[:, c, :], start=(c == 0), stop=(c == NC - 1))
            mm.then_inc(job_mm.sem, 1)

        def x_proj_small(pe, row, par, half):
            bank = job_bank(pe, row, par, SJ) if half == 0 else ring[:, (par + SJ) % 2, :]
            pe.wait_ge(xc_ready.sem, xc_ready.at(row, (half + 1) * ND // 2))
            for d in range(half * ND // 2, (half + 1) * ND // 2):
                mm = pe.matmul(bank[0:48, :], w_x[:, d, DI:], hx[:, d, :], start=(d == 0), stop=(d == ND - 1))
            if half == 1:
                mm.then_inc(job_mm.sem, 1)

        def x_proj(pe, row, par, m, half):
            bank = job_bank(pe, row, par, UJ[m]) if half == 0 else ring[:, (par + UJ[m]) % 2, :]
            for d in range(half * ND // 2, (half + 1) * ND // 2):
                mm = pe.matmul(bank, w_x[:, d, m * P:(m + 1) * P], hx[:, d, :], start=(d == 0), stop=(d == ND - 1))
            if half == 1:
                mm.then_inc(job_mm.sem, 1)

        def dt_proj(pe, row, par, m):
            bank = job_bank(pe, row, par, DJ + m)
            pe.wait_ge(job_ev.sem, job_ev.at(row, SJ + 1))
            pe.matmul(bank, w_dt[:, m * P:(m + 1) * P], db[0:32, :], start=True, stop=True).then_inc(job_mm.sem, 1)

        def sum_step(pe, row, s):
            g, dt, part = step_of(s)
            if s in ADDED:
                pe.wait_ge(added.sem, added.at(row, ADDED.index(s) + 1))
            else:
                pe.wait_ge(scanned.sem, scanned.at(row, s + 1))
            if g == 0 and part == 0:
                pe.wait_ge(ys_read.sem, ys_read.at(row - 1, dt + 1))
            terms = 1 if s in ADDED else SN
            for i in range(terms):
                mm = pe.matmul(ys[:, dt, :], k.ident[:], hs[:, s % DEEP, i, :], start=(g == 0 and part == 0 and i == 0),
                               stop=(g == NG - 1 and part == GN // SN - 1 and i == terms - 1))
            mm.then_inc(summed.sem, 1)

        def out_proj(pe, row, par, j):
            if j == 0:
                pe.wait_ge(y2_ready.sem, y2_ready.at(row, ND))
                pe.wait_ge(r.done.sem, r.done.at(row - 1, 1))
            h, q = j // 2, j % 2
            for d in range(ND):
                mm = pe.matmul(ob[:, h, q * C:(q + 1) * C], sz[:, par, d, j * P:(j + 1) * P], w_out[:, d, :],
                               start=(d == 0), stop=(d == ND - 1))
            if q == 1:
                mm.then_inc(o_mm.sem, 1)

        def rows(eng, one_row):
            one_row(0, 0)
            one_row(1, 1)
            with eng.Fori(1, B // 2 - 1) as pair:
                one_row(2 * pair, 0)
                one_row(2 * pair + 1, 1)
            one_row(B - 2, 0)
            one_row(B - 1, 1)

        def is_row(row, n):
            return isinstance(row, int) and row == n

        def last(row):
            return is_row(row, B - 1)

        def first(row):
            return is_row(row, 0)

        with nc.Block() as block:
            @block.sync
            def _(sp):
                load_x(sp, 0)
                load_first_consts(sp)
                load_consts(sp)
                load_x(sp, 1)
                store_b(sp, 0, 0)
                spread_b(sp, 0, 0, 0)

                def one_row(row, par):
                    spread_b(sp, row, par, 1)
                    if not (last(row) or is_row(row, B - 2)):
                        load_x(sp, row + 2)
                    spread_b(sp, row, par, 2)
                    if not first(row):
                        store_x1(sp, row - 1)
                    load_x1(sp, row)
                    spread_b(sp, row, par, 3)
                    if not last(row):
                        store_b(sp, row + 1, 1 - par)
                        spread_b(sp, row + 1, 1 - par, 0)
                    if first(row):
                        load_route_consts(sp)
                    if first(row) or is_row(row, 1):
                        clear_slots(sp, row)

                rows(sp, one_row)
                store_x1(sp, B - 1)
                sp.wait_ge(x1_st.sem, x1_st.at(B - 1, 16))
                sp.wait_ge(route_loaded, 16 * ROUTE_CONSTS)

            @block.gpsimd
            def _(pool):
                pool.memset(w_dt[:], 0.0).then_inc(dt_cleared, 1)
                pool.memset(b_db[:], 0.0).then_inc(bias_one, 1)
                pool.wait_ge(bias_one, 1)
                pool.affine_select(out=b_db[:], in_=b_db[:], compare_op=ALU.not_equal, fill=1.0, base=-NS,
                                   pattern=[[0, 1]], channel_multiplier=1).then_inc(bias_one, 1)
                pool.memset(w_x[:, :, DI + NS:DI + 32], 0.0).then_inc(cleared, 1)
                pool.memset(xc[:, :, 0:DC - 1], 0.0).then_inc(cleared, 1)
                norm_rstd(pool, norm, 0)
                pool.wait_ge(loaded, 16 * CONSTS)

                def one_row(row, par):
                    for s in range(STEPS):
                        input_step(pool, row, par, s)
                        if s == 4 and not last(row):
                            norm_rstd(pool, norm, row + 1)
                        if s == 20 and not first(row):
                            norm_rstd(pool, r.norm, row - 1)
                        if s == 22:
                            add_out_bias(pool, row)
                        if s == STEPS - 1 and is_row(row, 1):
                            pool.wait_ge(zeroed, 16 * ZN)
                        if 1 <= s < 1 + NT * K and not (first(row) or is_row(row, 1)):
                            route_send(pool, r, row - 2, s - 1)

                rows(pool, one_row)
                for n in range(NT * K):
                    route_send(pool, r, B - 2, n)
                norm_rstd(pool, r.norm, B - 1)
                for n in range(NT * K):
                    route_send(pool, r, B - 1, n)
                pool.wait_ge(r.sent.sem, r.sent.at(B - 1, 16 * NT * K))

            @block.scalar
            def _(act):
                act.wait_ge(first_loaded, 16 * FIRST_CONSTS)
                act.wait_ge(halved, 3)

                def first_part(row, par, s):
                    if s == 8:
                        for c in range(NC):
                            turned(act, row, par, c)
                    for m in range(ND):
                        if s == 9 + m:
                            conv_input(act, row, par, m)
                        if s == (9, 11, 13, 14)[m]:
                            conv_first(act, row, m)
                        if s == (12, 14, 16, 17)[m]:
                            tanh_x(act, row, m)
                    if s == 20:
                        delta_b(act, row, par)
                    if s == 22:
                        u_bias(act, row, par, 0)
                    if s in (23, 24):
                        for m in range((s - 23) * 2, (s - 22) * 2):
                            step_size(act, row, par, m)
                    if s == 25:
                        exp_part(act, row)
                    if s == 26:
                        log_part(act, row)
                    if s in (27, 30):
                        u_bias(act, row, par, s // 3 - 8)

                for s in range(STEPS):
                    if s == 16:
                        act.wait_ge(loaded, 16 * CONSTS)
                    first_part(0, 0, s)

                def one_row(row, par):
                    for s in range(STEPS):
                        decay_step(act, row, par, s)
                        if s == 0:
                            u_bias(act, row, par, ND - 1)
                        if 4 <= s < 4 + ND:
                            gate_input(act, row, par, s - 4)
                        if 8 <= s < 8 + ND:
                            tanh_z(act, row, par, s - 8)
                        if not last(row):
                            first_part(row + 1, 1 - par, s)
                        if not first(row):
                            if s == 24:
                                for c in range(NC):
                                    route_turned(act, r, row - 1, c)
                            if s == 31:
                                route_exp(act, r, row - 1)

                rows(act, one_row)
                for c in range(NC):
                    route_turned(act, r, B - 1, c)
                route_exp(act, r, B - 1)

            @block.vector
            def _(dve):
                dve.wait_ge(first_loaded, 16 * FIRST_CONSTS)
                dve.wait_ge(cleared, 2)
                dve.tensor_scalar(b_z[:], b_in[:, ND:], 0.5, None, ALU.mult).then_inc(halved, 1)
                dve.tensor_scalar(w_conv[:], w_conv[:], 0.5, None, ALU.mult).then_inc(halved, 1)
                dve.tensor_scalar(b_conv[:], b_conv[:], 0.5, None, ALU.mult).then_inc(halved, 1)
                dve.wait_ge(halved, 3)

                def first_part(row, par, s):
                    if s == 0:
                        dve.wait_ge(x_ld.sem, x_ld.at(row, 16))
                        norm_stats(dve, norm, xt, row)
                    if s == 3:
                        norm_apply(dve, norm, xt, xt, row)
                    for m in range(ND):
                        if s == (8, 10, 12, 13)[m]:
                            conv_step(dve, row, m)
                        if s == (10, 12, 14, 15)[m]:
                            silu_x(dve, row, m)
                        if s == 25 + m // 2:
                            softplus(dve, row, par, m)
                        if m < ND - 1 and s == 26 + 2 * m:
                            step_input(dve, row, par, m)

                for s in range(STEPS):
                    first_part(0, 0, s)
                dve.wait_ge(loaded, 16 * CONSTS)

                def one_row(row, par):
                    for s in range(STEPS):
                        scan_step(dve, row, s)
                        if s - 1 in ADDED:
                            add_states(dve, row, s - 1)
                        if s == 1:
                            step_input(dve, row, par, ND - 1)
                        for m in range(ND):
                            if s == (6, 7, 9, 11)[m]:
                                silu_z(dve, row, par, m)
                        if not first(row):
                            if s in (2, 4):
                                gate(dve, row - 1, 1 - par, ND - 3 + s // 2)
                            if s in (13, 15):
                                residual(dve, row - 1, (s - 13) // 2)
                            if s == 16:
                                route_stats(dve, row - 1)
                            if s == 19:
                                route_norm(dve, r, x1, row - 1)
                            if s == 27:
                                route_best(dve, r, row - 1)
                            if s == 30:
                                route_slots(dve, r, row - 1)
                        if not last(row):
                            first_part(row + 1, 1 - par, s)
                        if s in (28, 30):
                            gate(dve, row, par, (s - 28) // 2)

                rows(dve, one_row)
                for dt in (ND - 2, ND - 1):
                    gate(dve, B - 1, 1, dt)
                for h in range(2):
                    residual(dve, B - 1, h)
                route_stats(dve, B - 1)
                route_norm(dve, r, x1, B - 1)
                route_best(dve, r, B - 1)
                route_slots(dve, r, B - 1)

            @block.tensor
            def _(pe):
                pe.wait_ge(first_loaded, 16 * FIRST_CONSTS)
                pe.wait_ge(cleared, 1)

                def first_part(row, par, s):
                    if s == 4:
                        for c in range(NC):
                            turn(pe, row, par, c)
                    if 5 <= s < 5 + ND:
                        in_proj(pe, row, par, IJ + s - 5, s - 5)
                    if s in (15, 16):
                        x_proj_small(pe, row, par, s - 15)
                    if s in (17, 18):
                        x_proj(pe, row, par, 0, s - 17)
                    if s in (19, 20):
                        for m in range((s - 19) * 2, (s - 18) * 2):
                            dt_proj(pe, row, par, m)
                    for m in range(1, ND):
                        if s in (19 + 3 * m, 20 + 3 * m):
                            x_proj(pe, row, par, m, s - 19 - 3 * m)

                for s in range(STEPS):
                    if s == 15:
                        pe.wait_ge(loaded, 16 * CONSTS)
                    first_part(0, 0, s)

                def one_row(row, par):
                    for s in range(STEPS):
                        sum_step(pe, row, s)
                        if s < ND:
                            in_proj(pe, row, par, ZJ + s, ND + s)
                        if not first(row):
                            for j in range(NT):
                                if s == (9, 11, 12, 13)[j]:
                                    out_proj(pe, row - 1, 1 - par, j)
                            if s == 21:
                                for c in range(NC):
                                    route_transpose(pe, r, row - 1, c)
                            if s == 24 and is_row(row, 1):
                                pe.wait_ge(route_loaded, 16 * ROUTE_CONSTS)
                            if s == 24:
                                route_logits(pe, r, row - 1)
                            if s == 28:
                                route_places(pe, r, row - 1)
                        if not last(row):
                            first_part(row + 1, 1 - par, s)

                rows(pe, one_row)
                for j in range(NT):
                    out_proj(pe, B - 1, 1, j)
                for c in range(NC):
                    route_transpose(pe, r, B - 1, c)
                route_logits(pe, r, B - 1)
                route_places(pe, r, B - 1)


class Mixer:

    def __init__(self, sb, sem, name, k, copies, ahead, first=0):
        self.k, self.copies, self.first = k, copies, first
        self.index = sb(name + "_index", [P, copies, NT * K], U32)
        self.got, self.share = sb(name + "_got", [P, copies, NT * K, C]), sb(name + "_share", [P, NT * K])
        self.index_ready = Count(sem(name + "_index_ready"), 1)
        self.pool_held = sem(name + "_pool_held")
        self.fetched = [Count(sem(f"{name}_fetched{i}"), 16 * NT * K) for i in range(copies)]
        self.steps = Count(sem(name + "_steps"), 1 + NT * K, ahead)


def mix_fetch(pool, x, row, nth, copy, parts=range(NT * K)):
    turn = row - x.first
    if 0 in parts:
        mix_index(pool, x, row, turn, copy)
    for s in parts:
        pool.indirect_dma_start(x.got[:, copy, s, :], None, x.k.results,
                                bass.IndirectOffsetOnAxis(ap=x.index[:, copy, s:s + 1], axis=0),
                                bounds_check=SLOTS - 1, oob_is_err=False).then_inc(x.fetched[copy].sem, 16)


def mix_index(pool, x, row, turn, copy):
    pool.wait_ge(x.steps.sem, x.steps.at(turn - x.copies, 1 + NT * K))
    pool.tensor_copy(x.index[:, copy, :], x.k.fetch[:, bass.ds(row, 1), :].rearrange("p a s -> p (a s)")) \
        .then_inc(x.index_ready.sem, 1)
    pool.wait_ge(x.index_ready.sem, x.index_ready.at(turn, 1))
    pool.sem_inc(x.pool_held, 1)


def mix(dve, x, row, nth, copy, base, out, choices=range(K)):
    done, turn = x.steps, row - x.first
    if 0 in choices:
        mix_shares(dve, x, row, nth, copy)
    for kk in choices:
        dve.wait_ge(done.sem, done.at(turn, 1 + kk * NT))
        for j in range(NT):
            at = j * K + kk
            dve.scalar_tensor_tensor(out[:, j, :], x.got[:, copy, at, :], x.share[:, at:at + 1],
                                     (base if kk == 0 else out)[:, j, :], ALU.mult, ALU.add).then_inc(done.sem, 1)
    if K - 1 in choices:
        dve.wait_ge(done.sem, done.at(turn, 1 + NT * K))


def mix_shares(dve, x, row, nth, copy):
    done = x.steps
    dve.tensor_copy(x.share[:], x.k.share[:, bass.ds(row, 1), :].rearrange("p a s -> p (a s)")).then_inc(done.sem, 1)
    dve.wait_ge(x.fetched[copy].sem, x.fetched[copy].at(nth, 16 * NT * K))


def experts_phase(nc, k, w, name, out=None):
    with ExitStack() as ctx:
        def sb(n, shape, dt=F32):
            return ctx.enter_context(nc.sbuf_tensor(f"{name}_{n}", shape, dt))

        def sem(n):
            return ctx.enter_context(nc.semaphore(f"{name}_{n}"))

        TURNS = 2 * E
        HN = 2
        HW = ROWS // HN
        TJ = 3
        WP = 4
        HB = 4

        w1, w2 = sb("w1", [P, 2, NC, H]), sb("w2", [P, NH, C])
        w1_hi, w1_lo = (sb(n, [P, 2, NC, H], F32R) for n in ("w1_hi", "w1_lo"))
        w2_hi, w2_lo = (sb(n, [P, 2, NH, C], F32R) for n in ("w2_hi", "w2_lo"))
        b1, b2 = sb("b1", [P, 2, NH]), sb("b2", [P, 2, C])
        rows = sb("rows", [P, 2, NR, C])
        rowsT_hi, rowsT_lo = (sb(n, [P, NC, ROWS], F32R) for n in ("rowsT_hi", "rowsT_lo"))
        h = sb("h", [P, HB, ROWS])
        hT_hi, hT_lo = (sb(n, [P, NH, ROWS], F32R) for n in ("hT_hi", "hT_lo"))
        y = sb("y", [P, 2, NR, C])
        tbank = ctx.enter_context(nc.psum_tensor(name + "_tbank", [P, 2, 512], F32))
        hbank = ctx.enter_context(nc.psum_tensor(name + "_hbank", [P, 4, 512], F32))
        ybank = ctx.enter_context(nc.psum_tensor(name + "_ybank", [P, 2, 512], F32))

        if out is not None:
            xa, xo = sb("xa", [P, 2, NT, C]), sb("xo", [P, 2, NT, C])
            mixer = Mixer(sb, sem, "mix", k, 1, 1)
            x_ld = [Count(sem(f"x_ld{i}"), 16) for i in range(2)]
            xo_st = [Count(sem(f"xo_st{i}"), 16, ahead=1) for i in range(2)]

        w1_loaded, w2_loaded = [Count(sem(f"w1_loaded{i}"), 16) for i in range(2)], Count(sem("w2_loaded"), 16)
        loaded = [Count(sem(f"loaded{i}"), 32) for i in range(2)]
        w_hi, w_lo = Count(sem("w_hi"), 2 * WP), Count(sem("w_lo"), 2 * WP, ahead=2)
        stored, y_free = Count(sem("stored"), 16), Count(sem("y_free"), 1)
        b1_ready = Count(sem("b1_ready"), 1)
        t_mm, t_hi, t_lo = Count(sem("t_mm"), TJ), Count(sem("t_hi"), TJ), Count(sem("t_lo"), TJ, ahead=1)
        h_mm, h_ev = Count(sem("h_mm"), NH * HN), Count(sem("h_ev"), NH * HN, ahead=1)
        h_hi, h_lo = Count(sem("h_hi"), NH), Count(sem("h_lo"), NH, ahead=1)
        y_mm, y_ev = Count(sem("y_mm"), NR, ahead=2), Count(sem("y_ev"), NR, ahead=2)

        def load(sp, turn, par, e):
            sp.wait_ge(w_lo.sem, w_lo.at(turn - 2, WP))
            sp.dma_start(w1[:, par], w["W1"][e].rearrange("(k p) h -> p k h", p=P)).then_inc(w1_loaded[par].sem, 16)
            sp.wait_ge(y_ev.sem, y_ev.at(turn - 2, NR))
            for dst, src in ((rows[:, par], k.slots[bass.ds(turn * ROWS, ROWS)].rearrange("(r p) c -> p r c", p=P)),
                             (b2[:, par], w["b2"][e].partition_broadcast(P))):
                sp.dma_start(dst, src).then_inc(loaded[par].sem, 16)
            sp.wait_ge(w_lo.sem, w_lo.at(turn - 1, 2 * WP))
            sp.dma_start(w2[:], w["W2"][e].rearrange("(m p) c -> p m c", p=P)).then_inc(w2_loaded.sem, 16)

        def weight_piece(piece, par):
            if piece < WP:
                c, at = piece // (WP // NC), slice(piece % (WP // NC) * (H * NC // WP), (piece % (WP // NC) + 1) * (H * NC // WP))
                return w1[:, par, c, at], w1_hi[:, par, c, at], w1_lo[:, par, c, at]
            at = slice((piece - WP) * (NH // WP), (piece - WP + 1) * (NH // WP))
            return w2[:, at], w2_hi[:, par, at], w2_lo[:, par, at]

        def weight_high(act, turn, pair, par, piece):
            if piece == 0:
                act.wait_ge(w1_loaded[par].sem, w1_loaded[par].at(pair, 16))
            elif piece == WP:
                act.wait_ge(w2_loaded.sem, w2_loaded.at(turn, 16))
            act.wait_ge(y_mm.sem, y_mm.at(turn - 2, NR))
            full, high, low = weight_piece(piece, par)
            act.activation(high, full, ACT.Copy).then_inc(w_hi.sem, 1)

        def weight_low(pool, turn, par, piece):
            pool.wait_ge(w_hi.sem, w_hi.at(turn, piece + 1))
            full, high, low = weight_piece(piece, par)
            pool.tensor_tensor(low, full, high.bitcast(F32), ALU.subtract).then_inc(w_lo.sem, 1)

        def turn_rows(pe, turn, pair, par, jobs):
            if 0 in jobs:
                pe.wait_ge(loaded[par].sem, loaded[par].at(pair, 32))
            for job in jobs:
                if job < 2:
                    pe.wait_ge(t_lo.sem, t_lo.at(turn - 1, TJ - job))
                    for r in range(4):
                        mm = pe.transpose(tbank[:, job, r * P:(r + 1) * P], rows[:, par, r, job * P:(job + 1) * P],
                                          k.ident[:])
                else:
                    pe.wait_ge(t_lo.sem, t_lo.at(turn, 1))
                    for c in range(NC):
                        mm = pe.transpose(tbank[:, 0, c * P:(c + 1) * P], rows[:, par, 4, c * P:(c + 1) * P], k.ident[:])
                mm.then_inc(t_mm.sem, 1)

        def turned_part(t, job):
            if job < 2:
                return t[:, job, 0:512], tbank[:, job, :]
            return t[:, :, 512:ROWS], tbank[:, 0, 0:NC * P].rearrange("p (c t) -> p c t", t=P)

        def turned_high(act, turn, jobs=range(TJ)):
            for job in jobs:
                act.wait_ge(t_mm.sem, t_mm.at(turn, job + 1))
                high, bank = turned_part(rowsT_hi, job)
                act.activation(high, bank, ACT.Copy).then_inc(t_hi.sem, 1)

        def turned_low(dve, turn, jobs=range(TJ)):
            for job in jobs:
                dve.wait_ge(t_hi.sem, t_hi.at(turn, job + 1))
                high, bank = turned_part(rowsT_hi, job)
                low, bank = turned_part(rowsT_lo, job)
                dve.tensor_tensor(low, bank, high.bitcast(F32), ALU.subtract).then_inc(t_lo.sem, 1)

        def first_product(pe, turn, par):
            for m in range(NH):
                for n in range(HN):
                    job = m * HN + n
                    if job == 0:
                        pe.wait_ge(t_lo.sem, t_lo.at(turn, TJ))
                        pe.wait_ge(w_lo.sem, w_lo.at(turn, WP))
                    pe.wait_ge(h_ev.sem, h_ev.at(turn, job - 3))
                    for c in range(NC):
                        ws, rs = slice(m * P, (m + 1) * P), slice(n * HW, (n + 1) * HW)
                        pe.matmul(hbank[:, job % 4, 0:HW], w1_hi[:, par, c, ws], rowsT_hi[:, c, rs], start=(c == 0), stop=False)
                        pe.matmul(hbank[:, job % 4, 0:HW], w1_hi[:, par, c, ws], rowsT_lo[:, c, rs], start=False, stop=False)
                        mm = pe.matmul(hbank[:, job % 4, 0:HW], w1_lo[:, par, c, ws], rowsT_hi[:, c, rs], start=False,
                                       stop=(c == NC - 1))
                    mm.then_inc(h_mm.sem, 1)

        def relu(act, turn, par, m):
            for n in range(HN):
                job = m * HN + n
                act.wait_ge(h_lo.sem, h_lo.at(turn, m + 1 - HB))
                act.wait_ge(h_mm.sem, h_mm.at(turn, job + 1))
                act.activation(h[:, m % HB, n * HW:(n + 1) * HW], hbank[:, job % 4, 0:HW], ACT.Relu,
                               bias=b1[:, par, m:m + 1]).then_inc(h_ev.sem, 1)

        def split_hidden(dve, turn, m):
            dve.wait_ge(h_ev.sem, h_ev.at(turn, (m + 1) * HN))
            dve.tensor_copy(hT_hi[:, m, :], h[:, m % HB, :]).then_inc(h_hi.sem, 1)
            dve.wait_ge(h_hi.sem, h_hi.at(turn, m + 1))
            dve.tensor_tensor(hT_lo[:, m, :], h[:, m % HB, :], hT_hi[:, m, :].bitcast(F32),
                              ALU.subtract).then_inc(h_lo.sem, 1)

        def second_product(pe, turn, par, parts):
            if 0 in parts:
                pe.wait_ge(w_lo.sem, w_lo.at(turn, 2 * WP))
            for r in parts:
                pe.wait_ge(y_ev.sem, y_ev.at(turn, r - 1))
                for m in range(NH):
                    if r == 0:
                        pe.wait_ge(h_lo.sem, h_lo.at(turn, m + 1))
                    bank, rs = ybank[:, (par + r) % 2, 0:C], slice(r * P, (r + 1) * P)
                    pe.matmul(bank, hT_hi[:, m, rs], w2_hi[:, par, m, :], start=(m == 0), stop=False)
                    pe.matmul(bank, hT_hi[:, m, rs], w2_lo[:, par, m, :], start=False, stop=False)
                    mm = pe.matmul(bank, hT_lo[:, m, rs], w2_hi[:, par, m, :], start=False, stop=(m == NH - 1))
                mm.then_inc(y_mm.sem, 1)

        def second_bias(dve, turn, par, parts):
            if 0 in parts:
                dve.wait_ge(y_free.sem, y_free.at(turn - 1, 1))
            for r in parts:
                dve.wait_ge(y_mm.sem, y_mm.at(turn, r + 1))
                dve.tensor_tensor(y[:, par, r, :], ybank[:, (par + r) % 2, 0:C], b2[:, par, :],
                                  ALU.add).then_inc(y_ev.sem, 1)

        def store(pool, turn, par):
            pool.wait_ge(stored.sem, stored.at(turn - 1, 16))
            pool.sem_inc(y_free.sem, 1)
            pool.wait_ge(y_ev.sem, y_ev.at(turn, NR))
            pool.dma_start(k.results[bass.ds(turn * ROWS, ROWS)].rearrange("(r p) c -> p r c", p=P),
                           y[:, par]).then_inc(stored.sem, 16)

        def load_x(sp, row, nth, par):
            sp.wait_ge(mixer.steps.sem, mixer.steps.at(row - 2, 1 + NT * K))
            sp.dma_start(xa[:, par], k.x3[bass.ds(row, 1)].rearrange("a (j p) c -> p (a j) c", p=P)).then_inc(x_ld[par].sem, 16)

        def mix_row(dve, row, nth, par):
            dve.wait_ge(x_ld[par].sem, x_ld[par].at(nth, 16))
            dve.wait_ge(xo_st[par].sem, xo_st[par].at(nth - 1, 16))
            mix(dve, mixer, row, row, 0, xa[:, par], xo[:, par])

        def store_row(sp, row, par):
            sp.wait_ge(mixer.steps.sem, mixer.steps.at(row, 1 + NT * K))
            sp.dma_start(out[bass.ds(row, 1)].rearrange("a (j p) c -> p (a j) c", p=P), xo[:, par]).then_inc(xo_st[par].sem, 16)

        def turns(eng, one_turn):
            with eng.Fori(0, E // 2) as pair:
                one_turn(2 * pair, pair, 0, None)
                one_turn(2 * pair + 1, pair + 1, 1, None)
            with eng.Fori(E // 2, E - 1) as pair:
                one_turn(2 * pair, pair, 0, 2 * pair - E)
                one_turn(2 * pair + 1, pair + 1, 1, 2 * pair + 1 - E)
            one_turn(TURNS - 2, E - 1, 0, HALF - 2)
            one_turn(TURNS - 1, E, 1, HALF - 1)

        def last(turn):
            return isinstance(turn, int) and turn == TURNS - 1

        def mixes(row):
            return out is not None and row is not None

        with nc.Block() as block:
            @block.sync
            def _(sp):
                if out is not None:
                    for par in range(2):
                        xo_st[par].grant(sp)
                with sp.Fori(0, E // 2) as pair:
                    for par in range(2):
                        load(sp, pair * 2 + par, par, pair * 2 + par)
                for par in range(2):
                    load(sp, E + par, par, par)
                    if out is not None:
                        load_x(sp, par, 0, par)
                with sp.Fori(1, E // 2) as pair:
                    for par in range(2):
                        load(sp, E + pair * 2 + par, par, pair * 2 + par)
                        if out is not None:
                            load_x(sp, pair * 2 + par, pair, par)
                            store_row(sp, pair * 2 + par - 2, par)
                if out is not None:
                    for par in range(2):
                        store_row(sp, HALF - 2 + par, par)
                    for par in range(2):
                        sp.wait_ge(xo_st[par].sem, xo_st[par].at(HALF // 2 - 1, 16))

            @block.tensor
            def _(pe):
                y_mm.grant(pe)
                turn_rows(pe, 0, 0, 0, range(TJ))

                def one_turn(turn, next_pair, par, row):
                    first_product(pe, turn, par)
                    if not last(turn):
                        turn_rows(pe, turn + 1, next_pair, 1 - par, range(TJ - 1))
                    second_product(pe, turn, par, range(2))
                    if not last(turn):
                        turn_rows(pe, turn + 1, next_pair, 1 - par, range(TJ - 1, TJ))
                    second_product(pe, turn, par, range(2, NR))

                turns(pe, one_turn)

            @block.scalar
            def _(act):
                h_ev.grant(act)
                for piece in range(WP):
                    weight_high(act, 0, 0, 0, piece)
                turned_high(act, 0)
                for piece in range(WP, 2 * WP):
                    weight_high(act, 0, 0, 0, piece)

                def one_turn(turn, next_pair, par, row):
                    act.activation(b1[:, par, :], k.b1[:, bass.ds(turn, 1), :].rearrange("p a m -> p (a m)"),
                                   ACT.Copy).then_inc(b1_ready.sem, 1)
                    act.wait_ge(b1_ready.sem, b1_ready.at(turn, 1))
                    for m in range(NH):
                        relu(act, turn, par, m)
                        if not last(turn):
                            weight_high(act, turn + 1, next_pair, 1 - par, m)
                    if not last(turn):
                        turned_high(act, turn + 1)

                turns(act, one_turn)

            @block.vector
            def _(dve):
                t_lo.grant(dve)
                h_lo.grant(dve)
                y_ev.grant(dve)
                if out is not None:
                    mixer.steps.grant(dve)
                turned_low(dve, 0)

                def one_turn(turn, next_pair, par, row):
                    for m in range(NH):
                        split_hidden(dve, turn, m)
                    if not last(turn):
                        turned_low(dve, turn + 1, range(TJ - 1))
                    second_bias(dve, turn, par, range(2))
                    if not last(turn):
                        turned_low(dve, turn + 1, range(TJ - 1, TJ))
                    second_bias(dve, turn, par, range(2, NR))
                    if mixes(row):
                        mix_row(dve, row, next_pair - E // 2 - par, par)

                turns(dve, one_turn)

            @block.gpsimd
            def _(pool):
                w_lo.grant(pool)
                for piece in range(2 * WP):
                    weight_low(pool, 0, 0, piece)

                def one_turn(turn, next_pair, par, row):
                    if not last(turn):
                        for piece in range(WP):
                            weight_low(pool, turn + 1, 1 - par, piece)
                    if mixes(row):
                        pool.wait_ge(stored.sem, stored.at(turn - 1, 16))
                        mix_fetch(pool, mixer, row, row, 0)
                    if not last(turn):
                        for piece in range(WP, 2 * WP):
                            weight_low(pool, turn + 1, 1 - par, piece)
                    store(pool, turn, par)

                turns(pool, one_turn)
                pool.wait_ge(stored.sem, stored.at(TURNS - 1, 16))


def attention_phase(nc, k, w):
    with ExitStack() as ctx:
        def sb(name, shape, dt=F32):
            return ctx.enter_context(nc.sbuf_tensor("a_" + name, shape, dt))

        def sem(name):
            return ctx.enter_context(nc.semaphore("a_" + name))

        GAMMA = 1.0 / float(np.sqrt(np.float32(C)))
        wq, wk, wv = (sb(n, [P, NC, C]) for n in ("wq", "wk", "wv"))
        xa, x2 = sb("xa", [P, NT, C]), sb("x2", [P, 2, NT, C])
        wq_hi, wk_hi, wv_hi, wq_lo, wk_lo, wv_lo = (sb(n, [P, NC, C], F32R) for n in (
            "wq_hi", "wk_hi", "wv_hi", "wq_lo", "wk_lo", "wv_lo"))
        xn, xnT_hi, xnT_lo = sb("xn", [P, NT, C]), sb("xnT_hi", [P, NC, T], F32R), sb("xnT_lo", [P, NC, T], F32R)
        qT, kT, v = sb("qT", [P, NC, T]), sb("kT", [P, NC, T]), sb("v", [P, NT, C])
        top, bias = sb("top", [P, NT]), sb("bias", [P, NT])
        pr, prT = sb("pr", [P, 2, T]), sb("prT", [P, 2, T])
        total, inverse = sb("total", [P, NT]), sb("inverse", [P, NT])
        x3 = sb("x3", [P, NT, C])
        ring = ctx.enter_context(nc.psum_tensor("a_ring", [P, 2, T], F32))
        sbank = ctx.enter_context(nc.psum_tensor("a_sbank", [P, 2, T], F32))
        tbank = ctx.enter_context(nc.psum_tensor("a_tbank", [P, 2, T], F32))
        obank = ctx.enter_context(nc.psum_tensor("a_obank", [P, 2, T], F32))

        r = Router(sb, sem, k, [ring[:, 0, :], ring[:, 1, :]], ring[:, 0, :], ring[:, 0, P:], copies=2)
        mixer = Mixer(sb, sem, "mix", k, 1, 0)
        norm = Norm(sb, sem, k, "norm")
        loaded = sem("loaded")
        x_ld, x3_st = Count(sem("x_ld"), 16), Count(sem("x3_st"), 16)
        w_hi, w_lo = sem("w_hi"), sem("w_lo")
        t_mm, t_hi, t_ev = Count(sem("t_mm"), NC), Count(sem("t_hi"), NC), Count(sem("t_ev"), NC)
        QKV = 6
        qkv_mm, qkv_ev = Count(sem("qkv_mm"), QKV), Count(sem("qkv_ev"), QKV)
        s_mm, max_ready, exp_ready = Count(sem("s_mm"), NT), Count(sem("max_ready"), 2 * NT), Count(sem("exp_ready"), NT)
        p_mm, p_ev = Count(sem("p_mm"), NT), Count(sem("p_ev"), NT)
        o_mm, inv_ready, x3_ready = Count(sem("o_mm"), NT), Count(sem("inv_ready"), NT), Count(sem("x3_ready"), NT)

        NEXT_NORM, LAST_NORM = 0, 7

        def load_x(sp, row):
            sp.wait_ge(mixer.steps.sem, mixer.steps.at(row - 1, 1 + NT * K))
            sp.dma_start(xa[:], k.x1[row].rearrange("(j p) c -> p j c", p=P)).then_inc(x_ld.sem, 16)

        def store_x3(sp, row):
            sp.wait_ge(x3_ready.sem, x3_ready.at(row, NT))
            sp.dma_start(k.x3[row].rearrange("(j p) c -> p j c", p=P), x3[:]).then_inc(x3_st.sem, 16)

        def add_ffn(dve, row, par, choices=range(K)):
            if 0 in choices:
                dve.wait_ge(x_ld.sem, x_ld.at(row, 16))
            mix(dve, mixer, row, row, 0, xa, x2[:, par], choices)

        def row_max(dve, row, i):
            dve.wait_ge(s_mm.sem, s_mm.at(row, i + 1))
            dve.tensor_reduce(top[:, i:i + 1], sbank[:, i % 2, 0:(i + 1) * P], AX.X, ALU.max).then_inc(max_ready.sem, 1)
            dve.wait_ge(max_ready.sem, max_ready.at(row, 2 * i + 1))
            dve.tensor_scalar(bias[:, i:i + 1], top[:, i:i + 1], -GAMMA, None, ALU.mult).then_inc(max_ready.sem, 1)

        def add_attention(dve, row, par, i):
            dve.wait_ge(exp_ready.sem, exp_ready.at(row, i + 1))
            dve.reciprocal(inverse[:, i:i + 1], total[:, i:i + 1]).then_inc(inv_ready.sem, 1)
            dve.wait_ge(inv_ready.sem, inv_ready.at(row, i + 1))
            dve.wait_ge(x3_st.sem, x3_st.at(row - 1, 16))
            dve.wait_ge(o_mm.sem, o_mm.at(row, i + 1))
            dve.scalar_tensor_tensor(x3[:, i, :], obank[:, i % 2, 0:C], inverse[:, i:i + 1], x2[:, par, i, :],
                                     ALU.mult, ALU.add).then_inc(x3_ready.sem, 1)

        def probs_turned(act, row, i):
            act.wait_ge(p_mm.sem, p_mm.at(row, i + 1))
            if i < 2:
                act.wait_ge(o_mm.sem, o_mm.at(row - 1, i + 3))
            else:
                act.wait_ge(o_mm.sem, o_mm.at(row, i - 1))
            act.activation(prT[:, i % 2, 0:(i + 1) * P], tbank[:, i % 2, 0:(i + 1) * P], ACT.Copy).then_inc(p_ev.sem, 1)

        def qkv_copy(act, row, job):
            act.wait_ge(qkv_mm.sem, qkv_mm.at(row, job + 1))
            dst = (qT[:, job, :] if job < NC else kT[:, job - NC, :] if job < 2 * NC
                   else v[:, 2 * (job - 2 * NC):2 * (job - 2 * NC) + 2, :].rearrange("p j c -> p (j c)"))
            act.activation(dst, ring[:, bank_of(job), :], ACT.Copy).then_inc(qkv_ev.sem, 1)

        def weight_high(act, nth, w_hi_tile, w_tile):
            act.wait_ge(loaded, 48)
            act.activation(w_hi_tile[:], w_tile[:], ACT.Copy).then_inc(w_hi, 1)

        def weight_low(dve, nth, w_lo_tile, w_hi_tile, w_tile):
            dve.wait_ge(w_hi, nth + 1)
            dve.tensor_tensor(w_lo_tile[:], w_tile[:], w_hi_tile[:].bitcast(F32), ALU.subtract).then_inc(w_lo, 1)

        def turned_high(act, row, c):
            act.wait_ge(t_mm.sem, t_mm.at(row, c + 1))
            act.activation(xnT_hi[:, c, :], ring[:, c, :], ACT.Copy).then_inc(t_hi.sem, 1)

        def turned_low(dve, row, c):
            dve.wait_ge(t_hi.sem, t_hi.at(row, c + 1))
            dve.tensor_tensor(xnT_lo[:, c, :], ring[:, c, :], xnT_hi[:, c, :].bitcast(F32), ALU.subtract).then_inc(t_ev.sem, 1)

        def probs(act, row, i):
            act.wait_ge(max_ready.sem, max_ready.at(row, 2 * (i + 1)))
            if i < 2:
                act.wait_ge(p_mm.sem, p_mm.at(row - 1, i + 3))
            else:
                act.wait_ge(p_mm.sem, p_mm.at(row, i - 1))
            act.wait_ge(x3_ready.sem, x3_ready.at(row - 1, NT))
            act.activation(pr[:, i % 2, 0:(i + 1) * P], sbank[:, i % 2, 0:(i + 1) * P], ACT.Exp, bias=bias[:, i:i + 1],
                           scale=GAMMA, accum_out=total[:, i:i + 1]).then_inc(exp_ready.sem, 1)

        def bank_of(job):
            return job % 2 if job < 2 * NC else 1

        def qkv(pe, row, job):
            if job < 2:
                pe.wait_ge(t_ev.sem, t_ev.at(row, NC))
            else:
                pe.wait_ge(qkv_ev.sem, qkv_ev.at(row, job if job > 2 * NC else job - 1))
            if job == 2 * NC:
                pe.wait_ge(qkv_ev.sem, qkv_ev.at(row, job))
                pe.wait_ge(r.x_ev.sem, r.x_ev.at(row - 1, NC))
            bank = ring[:, bank_of(job), :]
            if job < 2 * NC:
                w_hi, w_lo, m = ((wq_hi, wq_lo), (wk_hi, wk_lo))[job // NC] + (job % NC,)
                for c in range(NC):
                    ws = slice(m * P, (m + 1) * P)
                    pe.matmul(bank, w_hi[:, c, ws], xnT_hi[:, c, :], start=(c == 0), stop=False)
                    pe.matmul(bank, w_hi[:, c, ws], xnT_lo[:, c, :], start=False, stop=False)
                    mm = pe.matmul(bank, w_lo[:, c, ws], xnT_hi[:, c, :], start=False, stop=(c == NC - 1))
            else:
                for q in range(2):
                    ts = slice((2 * (job - 2 * NC) + q) * P, (2 * (job - 2 * NC) + q + 1) * P)
                    for c in range(NC):
                        part = bank[:, q * C:(q + 1) * C]
                        pe.matmul(part, xnT_hi[:, c, ts], wv_hi[:, c, :], start=(c == 0), stop=False)
                        pe.matmul(part, xnT_hi[:, c, ts], wv_lo[:, c, :], start=False, stop=False)
                        mm = pe.matmul(part, xnT_lo[:, c, ts], wv_hi[:, c, :], start=False, stop=(c == NC - 1))
            mm.then_inc(qkv_mm.sem, 1)

        def scores(pe, row, i):
            if i == 0:
                pe.wait_ge(qkv_ev.sem, qkv_ev.at(row, 2 * NC))
            if i < 2:
                pe.wait_ge(exp_ready.sem, exp_ready.at(row - 1, i + 3))
            else:
                pe.wait_ge(exp_ready.sem, exp_ready.at(row, i - 1))
            bank = sbank[:, i % 2, :]
            pe.matmul(bank[:, 0:(i + 1) * P], k.identb[:], k.future[:, T - (i + 1) * P:], start=True, stop=False)
            for c in range(NC):
                mm = pe.matmul(bank[:, 0:(i + 1) * P], qT[:, c, i * P:(i + 1) * P], kT[:, c, 0:(i + 1) * P], start=False,
                               stop=(c == NC - 1))
            mm.then_inc(s_mm.sem, 1)

        def turn(pe, row, c):
            pe.wait_ge(norm.ready.sem, norm.ready.at(row, NT))
            pe.wait_ge(qkv_ev.sem, qkv_ev.at(row - 1, QKV))
            if c == 0:
                pe.wait_ge(r.steps.sem, r.steps.at(row - 2, PLACES))
            for j in range(NT):
                mm = pe.transpose(ring[:, c, j * P:(j + 1) * P], xn[:, j, c * P:(c + 1) * P], k.ident[:])
            mm.then_inc(t_mm.sem, 1)

        def turn_probs(pe, row, i):
            pe.wait_ge(exp_ready.sem, exp_ready.at(row, i + 1))
            if i < 2:
                pe.wait_ge(p_ev.sem, p_ev.at(row - 1, i + 3))
            else:
                pe.wait_ge(p_ev.sem, p_ev.at(row, i - 1))
            for j in range(i + 1):
                mm = pe.transpose(tbank[:, i % 2, j * P:(j + 1) * P], pr[:, i % 2, j * P:(j + 1) * P], k.ident[:])
            mm.then_inc(p_mm.sem, 1)

        def values(pe, row, i):
            if i == 0:
                pe.wait_ge(qkv_ev.sem, qkv_ev.at(row, QKV))
            pe.wait_ge(p_ev.sem, p_ev.at(row, i + 1))
            if i < 2:
                pe.wait_ge(x3_ready.sem, x3_ready.at(row - 1, i + 3))
            else:
                pe.wait_ge(x3_ready.sem, x3_ready.at(row, i - 1))
            for j in range(i + 1):
                mm = pe.matmul(obank[:, i % 2, 0:C], prT[:, i % 2, j * P:(j + 1) * P], v[:, j, :], start=(j == 0),
                               stop=(j == i))
            mm.then_inc(o_mm.sem, 1)

        def rows(eng, one_row):
            one_row(0, 0)
            one_row(1, 1)
            with eng.Fori(1, B // 2 - 1) as pair:
                one_row(2 * pair, 0)
                one_row(2 * pair + 1, 1)
            one_row(B - 2, 0)
            one_row(B - 1, 1)

        def is_row(row, n):
            return isinstance(row, int) and row == n

        with nc.Block() as block:
            @block.sync
            def _(sp):
                load_x(sp, 0)
                for t, n in ((wq, "w_q"), (wk, "w_k"), (wv, "w_v")):
                    sp.dma_start(t[:], w[n].rearrange("(k p) n -> p k n", p=P)).then_inc(loaded, 16)
                load_x(sp, 1)

                def one_row(row, par):
                    if not (is_row(row, B - 2) or is_row(row, B - 1)):
                        load_x(sp, row + 2)
                    store_x3(sp, row)

                rows(sp, one_row)
                sp.wait_ge(x3_st.sem, x3_st.at(B - 1, 16))

            @block.gpsimd
            def _(pool):
                mix_fetch(pool, mixer, 0, 0, 0)
                norm_rstd(pool, norm, 0)
                mix_fetch(pool, mixer, 1, 1, 0)

                def one_row(row, par):
                    if not (is_row(row, B - 2) or is_row(row, B - 1)):
                        mix_fetch(pool, mixer, row + 2, row + 2, 0)
                    for n in range(NT * K):
                        if n == NEXT_NORM and not is_row(row, B - 1):
                            norm_rstd(pool, norm, row + 1)
                        if n == LAST_NORM:
                            norm_rstd(pool, r.norm, row)
                        if not is_row(row, 0):
                            route_send(pool, r, row - 1, n, 1 - par)

                rows(pool, one_row)
                for n in range(NT * K):
                    route_send(pool, r, B - 1, n, 1)
                pool.wait_ge(r.sent.sem, r.sent.at(B - 1, 16 * NT * K))

            @block.scalar
            def _(act):
                for nth, tiles in enumerate(((wq_hi, wq), (wk_hi, wk), (wv_hi, wv))):
                    weight_high(act, nth, *tiles)
                for c in range(NC):
                    turned_high(act, 0, c)
                for job in range(2 * NC):
                    qkv_copy(act, 0, job)

                def one_row(row, par):
                    probs(act, row, 0)
                    probs(act, row, 1)
                    qkv_copy(act, row, 2 * NC)
                    if not is_row(row, 0):
                        route_exp(act, r, row - 1)
                    probs_turned(act, row, 0)
                    probs(act, row, 2)
                    qkv_copy(act, row, 2 * NC + 1)
                    probs_turned(act, row, 1)
                    probs_turned(act, row, 2)
                    probs(act, row, 3)
                    probs_turned(act, row, 3)
                    if not is_row(row, B - 1):
                        for c in range(NC):
                            turned_high(act, row + 1, c)
                        for job in range(2 * NC):
                            qkv_copy(act, row + 1, job)
                    for c in range(NC):
                        route_turned(act, r, row, c)

                rows(act, one_row)
                route_exp(act, r, B - 1)

            @block.vector
            def _(dve):
                add_ffn(dve, 0, 0)
                norm_stats(dve, norm, x2[:, 0], 0)
                for nth, tiles in enumerate(((wq_lo, wq_hi, wq), (wk_lo, wk_hi, wk), (wv_lo, wv_hi, wv))):
                    weight_low(dve, nth, *tiles)
                norm_apply(dve, norm, x2[:, 0], xn, 0)
                for c in range(NC):
                    turned_low(dve, 0, c)
                add_ffn(dve, 1, 1, range(1))

                def one_row(row, par):
                    row_max(dve, row, 0)
                    row_max(dve, row, 1)
                    if not is_row(row, B - 1):
                        add_ffn(dve, row + 1, 1 - par, range(1, K))
                    if not is_row(row, 0):
                        route_best(dve, r, row - 1)
                        route_slots(dve, r, row - 1)
                    row_max(dve, row, 2)
                    add_attention(dve, row, par, 0)
                    if not is_row(row, B - 1):
                        norm_stats(dve, norm, x2[:, 1 - par], row + 1)
                    row_max(dve, row, 3)
                    if not is_row(row, B - 1):
                        dve.wait_ge(t_mm.sem, t_mm.at(row, NC))
                        norm_apply(dve, norm, x2[:, 1 - par], xn, row + 1)
                    add_attention(dve, row, par, 1)
                    add_attention(dve, row, par, 2)
                    if not is_row(row, B - 1):
                        for c in range(NC):
                            turned_low(dve, row + 1, c)
                    add_attention(dve, row, par, 3)
                    dve.wait_ge(x3_ready.sem, x3_ready.at(row, NT))
                    norm_stats(dve, r.norm, x3, row)
                    route_norm(dve, r, x3, row, par)
                    if not (is_row(row, B - 2) or is_row(row, B - 1)):
                        add_ffn(dve, row + 2, par, range(1))

                rows(dve, one_row)
                route_best(dve, r, B - 1)
                route_slots(dve, r, B - 1)

            @block.tensor
            def _(pe):
                for c in range(NC):
                    turn(pe, 0, c)
                pe.wait_ge(w_lo, 3)
                for job in range(2 * NC):
                    qkv(pe, 0, job)

                def one_row(row, par):
                    scores(pe, row, 0)
                    scores(pe, row, 1)
                    if not is_row(row, 0):
                        route_logits(pe, r, row - 1)
                    qkv(pe, row, 2 * NC)
                    if not is_row(row, 0):
                        route_places(pe, r, row - 1)
                    turn_probs(pe, row, 0)
                    scores(pe, row, 2)
                    qkv(pe, row, 2 * NC + 1)
                    turn_probs(pe, row, 1)
                    values(pe, row, 0)
                    turn_probs(pe, row, 2)
                    scores(pe, row, 3)
                    values(pe, row, 1)
                    values(pe, row, 2)
                    turn_probs(pe, row, 3)
                    if not is_row(row, B - 1):
                        for c in range(NC):
                            turn(pe, row + 1, c)
                    values(pe, row, 3)
                    if not is_row(row, B - 1):
                        for job in range(2 * NC):
                            qkv(pe, row + 1, job)
                    for c in range(NC):
                        if is_row(row, B - 1):
                            pe.wait_ge(r.steps.sem, r.steps.at(row - 1, PLACES))
                        else:
                            pe.wait_ge(qkv_ev.sem, qkv_ev.at(row + 1, 2 * NC - 1 + c))
                        route_transpose(pe, r, row, c, par)

                rows(pe, one_row)
                route_logits(pe, r, B - 1)
                route_places(pe, r, B - 1)


def combine_phase(nc, k, out):
    with ExitStack() as ctx:
        def sb(name, shape, dt=F32):
            return ctx.enter_context(nc.sbuf_tensor("c_" + name, shape, dt))

        def sem(name):
            return ctx.enter_context(nc.semaphore("c_" + name))

        xa, xo = sb("xa", [P, 2, NT, C]), sb("xo", [P, 2, NT, C])
        mixer = Mixer(sb, sem, "mix", k, 2, 2, first=HALF)
        x_ld = [Count(sem(f"x_ld{i}"), 16) for i in range(2)]
        stored = [Count(sem(f"stored{i}"), 16, ahead=1) for i in range(2)]

        with nc.Block() as block:
            @block.sync
            def _(sp):
                with sp.Fori(0, HALF // 2) as pair:
                    for par in range(2):
                        turn = 2 * pair + par
                        sp.wait_ge(mixer.steps.sem, mixer.steps.at(turn - 2, 1 + NT * K))
                        sp.dma_start(xa[:, par], k.x3[bass.ds(turn + HALF, 1)].rearrange("a (j p) c -> p (a j) c", p=P)) \
                            .then_inc(x_ld[par].sem, 16)

            @block.gpsimd
            def _(pool):
                with pool.Fori(0, HALF // 2) as pair:
                    for par in range(2):
                        mix_fetch(pool, mixer, 2 * pair + par + HALF, pair, par)

            @block.vector
            def _(dve):
                mixer.steps.grant(dve)
                with dve.Fori(0, HALF // 2) as pair:
                    for par in range(2):
                        dve.wait_ge(x_ld[par].sem, x_ld[par].at(pair, 16))
                        dve.wait_ge(stored[par].sem, stored[par].at(pair - 1, 16))
                        mix(dve, mixer, 2 * pair + par + HALF, pair, par, xa[:, par], xo[:, par])

            @block.scalar
            def _(act):
                for par in range(2):
                    stored[par].grant(act)
                with act.Fori(0, HALF // 2) as pair:
                    for par in range(2):
                        turn = 2 * pair + par
                        act.wait_ge(mixer.steps.sem, mixer.steps.at(turn, 1 + NT * K))
                        act.dma_start(out[bass.ds(turn + HALF, 1)].rearrange("a (j p) c -> p (a j) c", p=P), xo[:, par]) \
                            .then_inc(stored[par].sem, 16)
                for par in range(2):
                    act.wait_ge(stored[par].sem, stored[par].at(HALF // 2 - 1, 16))


SHORT = {"L0_attn_a_": "", "L0_attn_b_": "", "L0_ffn_": ""}


def short(name):
    for head in SHORT:
        if name.startswith(head):
            return name[len(head):]
    return name


def build(nc, arrays):
    w = {}
    for name, a in arrays.items():
        w[short(name)] = nc.dram_tensor(name, a.shape, mybir.dt.from_np(a.dtype), kind="ExternalInput").ap()
    out = nc.dram_tensor("out", (B, T, C), F32, kind="ExternalOutput").ap()
    with ExitStack() as ctx:
        ctx.enter_context(nc.allow_non_contiguous_dma(reason="short bias vectors, once"))
        k = build_kit(nc, ctx, w)
        mamba_phase(nc, k, w)
        experts_phase(nc, k, w, "ffn1")
        attention_phase(nc, k, w)
        experts_phase(nc, k, w, "ffn2", out)
        combine_phase(nc, k, out)


def kernel(**inputs):
    import concourse.bacc as bacc
    from concourse.bass_utils import run_bass_kernel_spmd

    nc = bacc.Bacc("TRN2", target_bir_lowering=False, num_devices=1)
    arrays = {name: np.ascontiguousarray(a) for name, a in inputs.items()}
    build(nc, arrays)
    r = run_bass_kernel_spmd(nc, [arrays], core_ids=[0])
    return r.results[0]["out"]
```
